# Optimizing a Trainium2 kernel written in Bass

```python
import numpy as np
import jax
import jax.numpy as jnp

def _softmax(x, axis=-1):
    return jax.nn.softmax(x, axis=axis)

def _gelu(x):
    return jax.nn.gelu(x, approximate=True)

def _silu(x):
    return jax.nn.silu(x)

def _sigmoid(x):
    return jax.nn.sigmoid(x)

def _layernorm(x, axis=-1, eps=1e-05):
    m = jnp.mean(x, axis=axis, keepdims=True)
    v = jnp.var(x, axis=axis, keepdims=True)
    return (x - m) / jnp.sqrt(v + eps)

def _scatter_add(tgt, idx, src, axis=0):
    return tgt.at[idx].add(src)

def _segment_sum(src, seg, n):
    return jax.ops.segment_sum(src, seg, n)
kernel_name = 'mk_adaln_d1_jaxref_r8_eb1c79'

def setup_inputs(seed: int=0):
    np.random.seed(seed)
    _w = jnp.asarray

    def _L0_attn_setup():
        import jax, jax.numpy as jnp
        import numpy as np
        B, S, HID = (2, 512, 512)
        H, HKV, D = (32, 8, 128)
        G = H // HKV
        EPS = 1e-06

        def _reference_tuple_inner(hidden_states, Wq, bq, Wk, bk, Wv, bv, Wo, M, z):
            b, s, _ = hidden_states.shape
            q = (hidden_states @ Wq.T + bq).reshape(b, s, H, D)
            k = (hidden_states @ Wk.T + bk).reshape(b, s, HKV, D)
            v = (hidden_states @ Wv.T + bv).reshape(b, s, HKV, D)
            sig_q = jax.nn.elu(q) + 1.0
            sig_k = jax.nn.elu(k) + 1.0
            q_sel = sig_q[:, :, ::G, :]
            num = jnp.einsum('bshd,hde->bshe', q_sel, M)
            den = jnp.einsum('bshd,hd->bsh', q_sel, z)[..., None] + EPS
            retrieved = num / den
            out_heads = jnp.repeat(retrieved, G, axis=2)
            output = out_heads.reshape(b, s, H * D) @ Wo.T
            M_new = M + jnp.einsum('bshd,bshe->hde', sig_k, v)
            z_new = z + sig_k.sum(axis=(0, 1))
            return (output, M_new, z_new)
        key = jax.random.key(seed)
        ks = jax.random.split(key, 10)
        s = 0.02
        return {'hidden_states': jax.random.normal(ks[0], (B, S, HID), jnp.float32), 'Wq': jax.random.normal(ks[1], (H * D, HID), jnp.float32) * s, 'bq': jnp.zeros((H * D,), jnp.float32), 'Wk': jax.random.normal(ks[2], (HKV * D, HID), jnp.float32) * s, 'bk': jnp.zeros((HKV * D,), jnp.float32), 'Wv': jax.random.normal(ks[3], (HKV * D, HID), jnp.float32) * s, 'bv': jnp.zeros((HKV * D,), jnp.float32), 'Wo': jax.random.normal(ks[4], (HID, H * D), jnp.float32) * s, 'M': jax.random.normal(ks[5], (HKV, D, D), jnp.float32), 'z': jax.random.uniform(ks[6], (HKV, D), jnp.float32) * 100.0 + 1.0}
    _L0_attn_in = _L0_attn_setup()

    def _L0_ffn_setup():
        import jax, jax.numpy as jnp
        import numpy as np
        SCALING = 32.0 / 16.0
        key = jax.random.key(seed)
        ks = jax.random.split(key, 7)
        B, T, D, O, R, E = (4, 256, 512, 512, 16, 8)
        x = jax.random.normal(ks[0], (B, T, D), dtype=jnp.float32)
        base_W = jax.random.normal(ks[1], (O, D), dtype=jnp.float32) * D ** (-0.5)
        base_b = jax.random.normal(ks[2], (O,), dtype=jnp.float32) * 0.01
        router_W = jax.random.normal(ks[3], (2 * E - 1, D), dtype=jnp.float32) * D ** (-0.5)
        router_b = jax.random.normal(ks[4], (2 * E - 1,), dtype=jnp.float32) * 0.01
        A = jax.random.normal(ks[5], (E, R, D), dtype=jnp.float32) * D ** (-0.5)
        Bm = jax.random.normal(ks[6], (E, O, R), dtype=jnp.float32) * R ** (-0.5)
        assigned_idx = 0
        others = [i for i in range(E) if i != assigned_idx]
        expert_map = jnp.array([assigned_idx] * E + others, dtype=jnp.int32)
        return {'x': x, 'base_W': base_W, 'base_b': base_b, 'router_W': router_W, 'router_b': router_b, 'A': A, 'B': Bm, 'expert_map': expert_map}
    _L0_ffn_in = _L0_ffn_setup()
    _L0_c = _w((lambda *s: np.random.randn(*s).astype(np.float32) * 0.05)(2, 512))
    _L0_wmod = _w((lambda *s: np.random.randn(*s).astype(np.float32) * 0.05)(512, 6 * 512) * 512 ** (-0.5))
    _d = {'L0_attn_hidden_states': _L0_attn_in['hidden_states'], 'L0_attn_Wq': _L0_attn_in['Wq'], 'L0_attn_bq': _L0_attn_in['bq'], 'L0_attn_Wk': _L0_attn_in['Wk'], 'L0_attn_bk': _L0_attn_in['bk'], 'L0_attn_Wv': _L0_attn_in['Wv'], 'L0_attn_bv': _L0_attn_in['bv'], 'L0_attn_Wo': _L0_attn_in['Wo'], 'L0_attn_M': _L0_attn_in['M'], 'L0_attn_z': _L0_attn_in['z'], 'L0_ffn_base_W': _L0_ffn_in['base_W'], 'L0_ffn_base_b': _L0_ffn_in['base_b'], 'L0_ffn_router_W': _L0_ffn_in['router_W'], 'L0_ffn_router_b': _L0_ffn_in['router_b'], 'L0_ffn_A': _L0_ffn_in['A'], 'L0_ffn_B': _L0_ffn_in['B'], 'L0_ffn_expert_map': _L0_ffn_in['expert_map'], 'L0_c': _L0_c, 'L0_wmod': _L0_wmod}
    _x0 = _d['L0_attn_hidden_states']
    _d['L0_attn_hidden_states'] = jax.random.normal(jax.random.fold_in(jax.random.key(seed), 1), (2, 512, 512), dtype=_x0.dtype)
    del _x0
    return _d

def reference(L0_attn_hidden_states, L0_attn_Wq, L0_attn_bq, L0_attn_Wk, L0_attn_bk, L0_attn_Wv, L0_attn_bv, L0_attn_Wo, L0_attn_M, L0_attn_z, L0_ffn_base_W, L0_ffn_base_b, L0_ffn_router_W, L0_ffn_router_b, L0_ffn_A, L0_ffn_B, L0_ffn_expert_map, L0_c, L0_wmod):

    def _L0_attn_ref(hidden_states, Wq, bq, Wk, bk, Wv, bv, Wo, M, z):
        import jax, jax.numpy as jnp
        import numpy as np
        B, S, HID = (2, 512, 512)
        H, HKV, D = (32, 8, 128)
        G = H // HKV
        EPS = 1e-06

        def _reference_tuple_inner(hidden_states, Wq, bq, Wk, bk, Wv, bv, Wo, M, z):
            b, s, _ = hidden_states.shape
            q = (hidden_states @ Wq.T + bq).reshape(b, s, H, D)
            k = (hidden_states @ Wk.T + bk).reshape(b, s, HKV, D)
            v = (hidden_states @ Wv.T + bv).reshape(b, s, HKV, D)
            sig_q = jax.nn.elu(q) + 1.0
            sig_k = jax.nn.elu(k) + 1.0
            q_sel = sig_q[:, :, ::G, :]
            num = jnp.einsum('bshd,hde->bshe', q_sel, M)
            den = jnp.einsum('bshd,hd->bsh', q_sel, z)[..., None] + EPS
            retrieved = num / den
            out_heads = jnp.repeat(retrieved, G, axis=2)
            output = out_heads.reshape(b, s, H * D) @ Wo.T
            M_new = M + jnp.einsum('bshd,bshe->hde', sig_k, v)
            z_new = z + sig_k.sum(axis=(0, 1))
            return (output, M_new, z_new)
        return _reference_tuple_inner(hidden_states, Wq, bq, Wk, bk, Wv, bv, Wo, M, z)[0]

    def _L0_ffn_ref(x, base_W, base_b, router_W, router_b, A, B, expert_map):
        import jax, jax.numpy as jnp
        import numpy as np
        SCALING = 32.0 / 16.0
        E = A.shape[0]
        base_out = jnp.einsum('btd,od->bto', x, base_W) + base_b
        logits = jnp.einsum('btd,nd->btn', x, router_W) + router_b
        probs = jax.nn.softmax(logits, axis=-1)
        topk_p, topk_i = jax.lax.top_k(probs, E)
        mapped = expert_map[topk_i]
        onehot = (mapped[..., None] == jnp.arange(E)).astype(x.dtype)
        w = jnp.einsum('btk,btke->bte', topk_p, onehot)
        h = jnp.einsum('btd,erd->bter', x, A)
        lora = jnp.einsum('bter,eor->bto', h * w[..., None], B) * SCALING
        return base_out + lora
    x = L0_attn_hidden_states
    mod = (_silu(L0_c) @ L0_wmod).reshape(L0_c.shape[0], 6, 1, -1)
    sa, ca, ga, sb, cb, gb = (mod[:, 0], mod[:, 1], mod[:, 2], mod[:, 3], mod[:, 4], mod[:, 5])
    ga = (2 * (ga >= 0) - 1) * jnp.maximum(jnp.abs(ga), 0.25)
    gb = (2 * (gb >= 0) - 1) * jnp.maximum(jnp.abs(gb), 0.25)
    h = _layernorm(x, axis=-1) * (1 + ca) + sa
    x = x + ga * _L0_attn_ref(h, L0_attn_Wq, L0_attn_bq, L0_attn_Wk, L0_attn_bk, L0_attn_Wv, L0_attn_bv, L0_attn_Wo, L0_attn_M, L0_attn_z)
    h = _layernorm(x, axis=-1) * (1 + cb) + sb
    x = x + gb * _L0_ffn_ref(h, L0_ffn_base_W, L0_ffn_base_b, L0_ffn_router_W, L0_ffn_router_b, L0_ffn_A, L0_ffn_B, L0_ffn_expert_map)
    return x

_drawn_inputs = setup_inputs


def setup_inputs(seed=0):
    import zlib

    import numpy as np

    out = dict(_drawn_inputs(seed))
    spreads = {'L0_attn_bq': (0.0, 2.0), 'L0_attn_bk': (0.0, 0.1), 'L0_attn_bv': (0.0, 0.1)}
    factors = {'L0_attn_Wq': 64.0,
     'L0_attn_Wo': 58.747,
     'L0_attn_M': 60.314,
     'L0_attn_z': 64.0,
     'L0_ffn_base_b': 24.539,
     'L0_ffn_router_b': 34.725}
    for name, (base, spread) in spreads.items():
        noise = np.random.default_rng([zlib.crc32(name.encode()), seed]).standard_normal(out[name].shape)
        drawn = base * np.exp(spread * noise) if base else spread * noise
        out[name] = jnp.asarray(drawn.astype(out[name].dtype))
    for name, factor in factors.items():
        out[name] = (out[name] * factor).astype(out[name].dtype)
    return out
```

```python
from contextlib import ExitStack

import concourse.bass as bass
from concourse import mybir

F32 = mybir.dt.float32
F32R = mybir.dt.float32r
I32 = mybir.dt.int32
ALU = mybir.AluOpType
ACT = mybir.ActivationFunctionType
AX = mybir.AxisListType

P = 128
B, S, HID = 2, 512, 512
HEADS, D = 8, 128
G = 4
KC = HID // P
TILES = B * S // P
TPB = TILES // B
UNITS = B * HEADS
E, R = 8, 16
NR = 2 * E - 1
ER = E * R
FW = HID + ER + NR + 1
FH = FW // 2
FB = HID - FH
EPS_DEN = 1e-6
EPS_LN = 1e-5
GATE_MIN = 0.25
SCALING = 2.0
RING = 3
SLOT = G * HID
MODS = [("sa", 0), ("ca", 1), ("ga", 2), ("gb", 5), ("sb", 3), ("cb", 4)]
ITEMS = ["mod0", "mod1", "wq0", "wq1", "mod2", "mod3", "mod4", "mod5"] + [f"wo{h}" for h in range(HEADS)] \
    + ["fw0", "fw1", "lb"]


def build(nc, x_d, c_d, wmod_d, wq_d, bq_d, z_d, wo_d, m_d, fw_d, lb_d, bb_d, rb_d, map_d, out_d):
    with ExitStack() as ctx:
        def sb(name, shape, dt=F32):
            return ctx.enter_context(nc.sbuf_tensor(name, shape, dt))

        def sem(name):
            return ctx.enter_context(nc.semaphore(name))

        x_sb = sb("x_sb", [P, TILES, HID])
        hn = sb("hn", [P, 2, HID])
        hfull = sb("hfull", [P, 2, KC, P])
        HT = sb("HT", [P, B, 2, KC, S], F32R)
        WQ = sb("WQ", [P, 2, HEADS, KC, D], F32R)
        sig, ql = [], []
        for b in range(B):
            at = nc.sbuf_base
            sig.append(sb(f"sig{b}", [P, HEADS, S]))
            ql.append(nc.alloc_sbuf_tensor_at(f"ql{b}", [P, HEADS, S], F32R, offset=at))
        MW = sb("MW", [P, 2, HEADS, HID], F32R)
        ring = sb("ring", [P, RING, SLOT])
        mT = sb("mT", [P, HEADS, D])
        lb_hi = sb("lb_hi", [P, HID], F32R)
        ident = sb("ident", [P, P])
        zcol = sb("zcol", [P, HEADS, 32])
        rfull = sb("rfull", [P, S])
        rrow = sb("rrow", [P, S], F32R)
        gates = sb("gates", [P, 2, B, HID])
        mrow = sb("mrow", [P, HID])
        et = sb("et", [P, 2, S])
        brow = sb("brow", [P, FW], F32R)
        pick = sb("pick", [P, HEADS], F32R)
        pick_b = sb("pick_b", [P, 2], F32R)
        msk = sb("msk", [P, 8])
        sct = sb("sct", [P, KC, 32])
        cin = sb("cin", [P, KC, B])
        ce = sb("ce", [P, 3, KC, B])
        zin = sb("zin", [P, HEADS])
        bqs = sb("bqs", [P, 3, HEADS])
        mods = sb("mods", [P, 4, KC, B])
        stat = sb("stat", [P, TILES, 2, 6])
        mv = sb("mv", [P, 2, TILES, 2])
        rs = sb("rs", [P, 2, 8, TILES])
        mapi = sb("mapi", [P, NR], I32)
        mapf = sb("mapf", [P, NR])
        oneh = sb("oneh", [P, E, NR])
        sm = sb("sm", [P, 2, 4, 16])
        sms = sb("sms", [P, 2, 4, 8])
        wt = sb("wt", [P, E, NR])
        hw = rfull[:, 0:ER]
        hwT = rrow[:, 0:2 * P].rearrange("p (l t) -> p l t", l=2)
        HTf = HT[:, :, :, :, :].rearrange("p b l k s -> p b (l k s)")
        WQf = WQ[:, :, :, :, :].rearrange("p l h k d -> p (l h k d)")
        qhi = [HTf[:, 0, :].rearrange("p (h s) -> p h s", h=HEADS),
               WQf[:, 0:HEADS * S].rearrange("p (h s) -> p h s", h=HEADS)]
        h2 = HTf[:, 1, 0:2 * 2 * HID].rearrange("p (a l k t) -> p a l k t", a=2, l=2, k=KC)
        fhi = WQf[:, HEADS * S:HEADS * S + KC * FW].rearrange("p (k n) -> p k n", k=KC)
        flo3 = HTf[:, 1, 4 * HID:4 * HID + 3 * FW].rearrange("p (k n) -> p k n", k=3)
        flo1 = WQf[:, HEADS * S + KC * FW:HEADS * S + (KC + 1) * FW]
        lbs = [lb_hi[:, :], WQf[:, HEADS * S + (KC + 1) * FW:HEADS * S + (KC + 1) * FW + HID]]
        braw = et[:, :, :].rearrange("p a s -> p (a s)")[:, 0:FW]

        def flo(k):
            return flo3[:, k, :] if k < 3 else flo1

        bank = [ctx.enter_context(nc.psum_tensor(f"bank{i}", [P, 512], F32)) for i in range(8)]
        ps_main = [bank[0], bank[1]]
        ps_den = bank[2]
        ps_bc = [bank[3], bank[4]]
        ps_t = [bank[5], bank[6]]
        ps_mod = bank[7]
        ps_ffn = [[bank[5], bank[6]], [bank[3], bank[4]]]

        x_in = [sem(f"x_in{t}") for t in range(TILES)]
        ring_in = [sem(f"ring_in{s}") for s in range(RING)]
        c_in, z_in, bq_in, m_in, map_in = sem("c_in"), sem("z_in"), sem("bq_in"), sem("m_in"), sem("map_in")
        bias_in = sem("bias_in")
        const = sem("const")
        ec_ready, silu_ready = sem("ec_ready"), sem("silu_ready")
        setup = sem("setup")
        mask_ready, zcol_ready = sem("mask_ready"), sem("zcol_ready")
        mod_done, mrow_ready, modT_done, mods_ready = sem("mod_done"), sem("mrow_ready"), sem("modT_done"), sem("mods_ready")
        gate_done, gate_ready = sem("gate_done"), sem("gate_ready")
        gate_tmp = sem("gate_tmp")
        st_ready, var_ready, ln_ready, y0_ready, newton = sem("st_ready"), sem("var_ready"), sem("ln_ready"), sem("y0_ready"), sem("newton")
        hn_ready, t_done, full_ready, hi_ready, lo_ready = sem("hn_ready"), sem("t_done"), sem("full_ready"), sem("hi_ready"), sem("lo_ready")
        wqh_ready, wql_ready = sem("wqh_ready"), sem("wql_ready")
        q_done, neg_ready, e_ready, bq_ready, sig_ready = sem("q_done"), sem("neg_ready"), sem("e_ready"), sem("bq_ready"), sem("sig_ready")
        den_done, r_ready, rrow_ready = sem("den_done"), sem("r_ready"), sem("rrow_ready")
        bc_done, qn_ready, qh_act, qh_pool, ql_ready = sem("bc_done"), sem("qn_ready"), sem("qh_act"), sem("qh_pool"), sem("ql_ready")
        woa_ready, wos_ready, mw_done, mwh_ready, mwl_ready = sem("woa_ready"), sem("wos_ready"), sem("mw_done"), sem("mwh_ready"), sem("mwl_ready")
        fwh_ready, fwl_ready, lbh_ready, lbl_ready = sem("fwh_ready"), sem("fwl_ready"), sem("lbh_ready"), sem("lbl_ready")
        o_done, og_ready, x2_ready = sem("o_done"), sem("og_ready"), sem("x2_ready")
        f_done, rmax_ready, rexp_ready, route, hw_ready = sem("f_done"), sem("rmax_ready"), sem("rexp_ready"), sem("route"), sem("hw_ready")
        hwT_done, hwh_ready, hwl_ready, l_done = sem("hwT_done"), sem("hwh_ready"), sem("hwl_ready"), sem("l_done")
        fg_ready, res_ready, out_in = sem("fg_ready"), sem("res_ready"), sem("out_in")
        block = ctx.enter_context(nc.Block())

        item = {name: i for i, name in enumerate(ITEMS)}

        def slot(name):
            return item[name] % RING

        def landed(eng, name):
            eng.wait_ge(ring_in[item[name] % RING], 16 * (item[name] // RING + 1))

        @block.sync
        def _(sp):
            def released(name):
                i = int(name[-1]) if name != "lb" else 0
                if name.startswith("mod"):
                    sp.wait_ge(mod_done, i + 1)
                elif name.startswith("wq"):
                    sp.wait_ge(wqh_ready, 4 * i + 4)
                    sp.wait_ge(wql_ready, 4 * i + 4)
                elif name.startswith("wo"):
                    sp.wait_ge(mw_done, i + 1)
                elif name.startswith("fw"):
                    sp.wait_ge(fwh_ready, i + 1)
                    sp.wait_ge(fwl_ready, 2 * i + 2)

            def load(name):
                n = item[name]
                if n >= RING:
                    released(ITEMS[n - RING])
                dst = ring[:, n % RING, :]
                i = int(name[-1]) if name != "lb" else 0
                if name.startswith("mod"):
                    src = wmod_d[MODS[i][1]]
                elif name.startswith("wq"):
                    src = wq_d[i]
                elif name.startswith("wo"):
                    src = wo_d[i]
                elif name.startswith("fw"):
                    dst = dst[:, 0:2 * FW].rearrange("p (k n) -> p k n", k=2)[:, :, 0:FW - 1]
                    src = fw_d[:, 2 * i:2 * i + 2, :]
                else:
                    dst, src = dst[:, 0:HID], lb_d
                sp.dma_start(dst, src).then_inc(ring_in[n % RING], 16)

            sp.dma_start(cin[:, :, :], c_d).then_inc(c_in, 16)
            for t in range(TPB):
                sp.dma_start(x_sb[:, t, :], x_d[t]).then_inc(x_in[t], 16)
            load("mod0")
            load("mod1")
            load("wq0")
            sp.dma_start(bqs[:, 0, :], bq_d).then_inc(bq_in, 16)
            sp.dma_start(zin[:, :], z_d).then_inc(z_in, 16)
            for t in range(TPB, TILES):
                sp.dma_start(x_sb[:, t, :], x_d[t]).then_inc(x_in[t], 16)
            load("wq1")
            sp.dma_start(mT[:, :, :], m_d).then_inc(m_in, 16)
            sp.dma_start(mapi[:, :], map_d.broadcast_to([P, NR])).then_inc(map_in, 16)
            for name in ITEMS[4:]:
                load(name)
            for t in range(TILES):
                sp.wait_ge(res_ready, t + 1)
                sp.dma_start(out_d[t], x_sb[:, t, :]).then_inc(out_in, 16)
            sp.wait_ge(out_in, 16 * TILES)

        @block.gpsimd
        def _(pool):
            pool.memset(sct[:, :, :], 0.0).then_inc(const, 1)
            pool.memset(ident[:, :], 0.0).then_inc(const, 1)
            pool.wait_ge(const, 2)
            pool.affine_select(out=ident[:, :], in_=ident[:, :], compare_op=ALU.not_equal, fill=1.0, base=0,
                               pattern=[[-1, P]], channel_multiplier=1).then_inc(const, 1)
            pool.memset(zcol[:, :, :], 0.0).then_inc(const, 1)
            pool.memset(braw, 0.0).then_inc(const, 1)
            pool.wait_ge(const, 5)
            for p in (0, 32):
                pool.dma_start(braw[p:p + 1, 0:HID], bb_d).then_inc(bias_in, 16)
                pool.dma_start(braw[p:p + 1, HID + ER:HID + ER + NR], rb_d).then_inc(bias_in, 16)

            def wq_hi(h):
                if h % 4 == 0:
                    landed(pool, f"wq{h // 4}")
                src = ring[:, slot(f"wq{h // 4}"), :].rearrange("p (h n) -> p h n", h=4)[:, h % 4, :]
                pool.tensor_scalar(WQ[:, 0, h, :, :].rearrange("p k d -> p (k d)"), src, 1.0, 1.0,
                                   ALU.mult, ALU.mult).then_inc(wqh_ready, 1)

            def q_hi(n):
                b, h = divmod(n, HEADS)
                if h == 1:
                    pool.wait_ge(q_done, HEADS * (b + 1))
                pool.wait_ge(qn_ready, n + 1)
                pool.tensor_scalar(qhi[b][:, h, :], sig[b][:, h, :], 1.0, 1.0, ALU.mult, ALU.mult).then_inc(qh_pool, 1)

            def wo_add(h):
                landed(pool, f"wo{h}")
                w = ring[:, slot(f"wo{h}"), :]
                pool.tensor_tensor(w[:, 0:2 * HID], w[:, 0:2 * HID], w[:, 2 * HID:4 * HID], ALU.add).then_inc(woa_ready, 1)

            for h in range(3):
                wq_hi(h)
            for u in range(UNITS):
                if u + 3 < HEADS:
                    wq_hi(u + 3)
                if 8 <= u < 15:
                    wo_add(u - 8)
                if u >= 12:
                    q_hi(2 * (u - 12) + 1)
            wo_add(7)
            pool.wait_ge(q_done, UNITS)
            pool.memset(fhi[:, :, FW - 1:FW].bitcast(F32), 0.0).then_inc(const, 1)
            pool.memset(flo3[:, :, FW - 1:FW].bitcast(F32), 0.0).then_inc(const, 1)
            pool.memset(flo1[:, FW - 1:FW].bitcast(F32), 0.0).then_inc(const, 1)
            for i in range(2):
                landed(pool, f"fw{i}")
                src = ring[:, slot(f"fw{i}"), 0:2 * FW].rearrange("p (k n) -> p k n", k=2)[:, :, 0:FW - 1]
                pool.tensor_scalar(fhi[:, 2 * i:2 * i + 2, 0:FW - 1], src, 1.0, 1.0, ALU.mult, ALU.mult).then_inc(fwh_ready, 1)
            landed(pool, "lb")
            pool.tensor_scalar(lbs[0], ring[:, slot("lb"), 0:HID], 1.0, 1.0, ALU.mult, ALU.mult).then_inc(lbh_ready, 1)
            for n in range(HEADS + 1, UNITS, 2):
                q_hi(n)

        @block.scalar
        def _(act):
            act.wait_ge(c_in, 16)
            act.activation(ce[:, 0, :, :], cin[:, :, :], ACT.Exp, scale=-1.0).then_inc(ec_ready, 1)

            def mod_evac(i):
                act.wait_ge(mod_done, i + 1)
                if i >= 1:
                    act.wait_ge(modT_done, [0, 1, 2, 2, 2, 3][i])
                    act.wait_ge(gate_done, [0, 0, 0, 2, 4, 4][i])
                act.activation(mrow[:, :], ps_mod[:, :], ACT.Copy).then_inc(mrow_ready, 1)

            def rsqrt_start(n, layer, lo, hi):
                act.wait_ge(var_ready, n + 1)
                act.activation(rs[:, layer, 1, lo:hi], rs[:, layer, 0, lo:hi], ACT.Ln).then_inc(ln_ready, 1)
                act.wait_ge(ln_ready, n + 1)
                act.activation(rs[:, layer, 2, lo:hi], rs[:, layer, 1, lo:hi], ACT.Exp, scale=-0.5).then_inc(y0_ready, 1)

            def modulate(n, layer, t, src, dst_hi):
                act.wait_ge(t_done, n + 1)
                act.wait_ge(mods_ready, 2 * layer + 2)
                if n >= 2:
                    act.wait_ge(lo_ready, n - 1)
                b = t // TPB
                for k in range(KC):
                    ins = act.activation(hfull[:, n % 2, k, :], src[:, k * P:(k + 1) * P], ACT.Identity,
                                         bias=mods[:, 2 * layer, k, b:b + 1], scale=mods[:, 2 * layer + 1, k, b:b + 1])
                ins.then_inc(full_ready, 1)
                act.wait_ge(full_ready, n + 1)
                act.activation(dst_hi, hfull[:, n % 2, :, :], ACT.Copy).then_inc(hi_ready, 1)

            def ln1_tile(t):
                modulate(t, 0, t, ps_t[t % 2], HT[:, t // TPB, 0, :, (t % TPB) * P:(t % TPB + 1) * P])

            def exp_q(u):
                act.wait_ge(q_done, u + 1)
                if u == 0:
                    act.wait_ge(bq_ready, 1)
                    act.wait_ge(mask_ready, 1)
                if u >= 2:
                    act.wait_ge(sig_ready, u - 1)
                h = u % HEADS
                act.activation(et[:, u % 2, :], ps_main[u % 2][:, :], ACT.Relu, bias=bqs[:, 2, h:h + 1], scale=-1.0).then_inc(neg_ready, 1)
                act.wait_ge(neg_ready, u + 1)
                act.activation(et[:, u % 2, :], et[:, u % 2, :], ACT.Exp, scale=-1.0).then_inc(e_ready, 1)

            def q_hi(n):
                b, h = divmod(n, HEADS)
                if h == 0:
                    act.wait_ge(q_done, HEADS * (b + 1))
                act.wait_ge(qn_ready, n + 1)
                act.activation(qhi[b][:, h, :], sig[b][:, h, :], ACT.Copy).then_inc(qh_act, 1)

            def mw_hi(h):
                act.wait_ge(mw_done, h + 1)
                act.activation(MW[:, 0, h, :], ps_t[h % 2][:, :], ACT.Copy).then_inc(mwh_ready, 1)

            rsqrt_start(0, 0, 0, TPB)
            mod_evac(0)
            mod_evac(1)
            for t in range(TPB):
                ln1_tile(t)
            rsqrt_start(1, 0, TPB, TILES)
            for u in range(UNITS):
                exp_q(u)
                if u < 2:
                    ln1_tile(TPB + 2 * u)
                    ln1_tile(TPB + 2 * u + 1)
                if u in (3, 5, 7, 9):
                    mod_evac(2 + (u - 3) // 2)
                if u >= 11:
                    mw_hi(u - 11)
                if u >= 12:
                    q_hi(2 * (u - 12))
            for h in range(5, HEADS):
                mw_hi(h)

            for s in range(TILES + 3):
                if s in (1, 2):
                    q_hi(4 + 4 * s)
                    q_hi(6 + 4 * s)
                if 0 <= s - 3 < TILES:
                    act.wait_ge(hwT_done, s - 2)
                    if s - 3 >= 1:
                        act.wait_ge(l_done, s - 3)
                    act.activation(hwT[:, 0, :], ps_mod[:, 0:P], ACT.Copy).then_inc(hwh_ready, 1)
                if 0 <= s - 1 < TILES:
                    t = s - 1
                    if t >= 2:
                        act.wait_ge(f_done, t - 1)
                    modulate(TILES + t, 1, t, ps_den, h2[:, t % 2, 0, :, :])
                if s < TILES:
                    rsqrt_start(2 + s, 1, s, s + 1)
                if 0 <= s - 2 < TILES:
                    t = s - 2
                    act.wait_ge(rmax_ready, t + 1)
                    act.activation(sm[:, t % 2, 0, 0:NR], ps_ffn[t % 2][1][:, FB + ER:FB + ER + NR], ACT.Exp,
                                   bias=sms[:, t % 2, 0, 0:1], accum_out=sms[:, t % 2, 0, 1:2]).then_inc(rexp_ready, 1)

        @block.vector
        def _(dve):
            steps = [0]

            def step(ins):
                steps[0] += 1
                ins.then_inc(setup, 1)
                dve.wait_ge(setup, steps[0])

            dve.wait_ge(ec_ready, 1)
            step(dve.tensor_scalar(ce[:, 1, :, :], ce[:, 0, :, :], 1.0, None, ALU.add))
            step(dve.reciprocal(ce[:, 2, :, :], ce[:, 1, :, :]))
            dve.wait_ge(const, 1)
            dve.tensor_tensor(sct[:, :, 0:B], cin[:, :, :], ce[:, 2, :, :], ALU.mult).then_inc(silu_ready, 1)

            def stats(n, layer, t):
                dve.bn_stats(stat[:, t, layer, :], x_sb[:, t, :]).then_inc(st_ready, 1)
                dve.wait_ge(st_ready, 2 * n + 1)
                dve.bn_aggr(mv[:, layer, t, :], stat[:, t, layer, :]).then_inc(st_ready, 1)

            def var_eps(n, layer, lo, hi):
                dve.wait_ge(st_ready, 2 * n)
                dve.tensor_scalar(rs[:, layer, 0, lo:hi], mv[:, layer, lo:hi, 1], EPS_LN, None, ALU.add).then_inc(var_ready, 1)

            def rsqrt_finish(n, layer, lo, hi):
                y0, v = rs[:, layer, 2, lo:hi], rs[:, layer, 0, lo:hi]
                dve.wait_ge(y0_ready, n + 1)
                step(dve.tensor_tensor(rs[:, layer, 3, lo:hi], y0, y0, ALU.mult))
                step(dve.tensor_tensor(rs[:, layer, 4, lo:hi], rs[:, layer, 3, lo:hi], v, ALU.mult))
                step(dve.tensor_scalar(rs[:, layer, 5, lo:hi], rs[:, layer, 4, lo:hi], -0.5, 1.5, ALU.mult, ALU.add))
                dve.tensor_tensor(rs[:, layer, 6, lo:hi], rs[:, layer, 5, lo:hi], y0, ALU.mult).then_inc(newton, 1)
                dve.wait_ge(newton, n + 1)

            def apply(n, layer, t):
                if n >= 2:
                    dve.wait_ge(t_done, n - 1)
                dve.tensor_scalar(hn[:, n % 2, :], x_sb[:, t, :], mv[:, layer, t, 0:1], rs[:, layer, 6, t:t + 1],
                                  ALU.subtract, ALU.mult).then_inc(hn_ready, 1)

            def split_lo(n, dst):
                dve.wait_ge(hi_ready, n + 1)
                src = hfull[:, n % 2, :, :]
                return dve.tensor_tensor(dst[1], src, dst[0].bitcast(F32), ALU.subtract).then_inc(lo_ready, 1)

            def ln1_lo(t):
                split_lo(t, [HT[:, t // TPB, l, :, (t % TPB) * P:(t % TPB + 1) * P] for l in range(2)])

            def wq_lo(h):
                dve.wait_ge(wqh_ready, h + 1)
                src = ring[:, slot(f"wq{h // 4}"), :].rearrange("p (h n) -> p h n", h=4)[:, h % 4, :]
                hi, lo = (WQ[:, l, h, :, :].rearrange("p k d -> p (k d)") for l in range(2))
                dve.tensor_tensor(lo, src, hi.bitcast(F32), ALU.subtract).then_inc(wql_ready, 1)

            def mod_finish(i, n):
                dve.wait_ge(modT_done, n + 1)
                src = ps_mod[:, :].rearrange("p (k q r) -> p k r q", k=KC, q=4)[:, :, 0:B, :]
                dst = mods[:, i, :, :]
                if i % 2 == 0:
                    dve.tensor_reduce(dst, src, AX.X, ALU.add).then_inc(mods_ready, 1)
                else:
                    step(dve.tensor_reduce(dst, src, AX.X, ALU.add))
                    dve.tensor_scalar(dst, dst, 1.0, None, ALU.add).then_inc(mods_ready, 1)

            def gate_finish(n):
                dve.wait_ge(gate_done, n + 1)
                src = ps_den if n % 2 == 0 else ps_mod
                g, b = divmod(n, 2)
                dst = gates[:, g, b, :]
                step(dve.tensor_scalar(dst, src[:, :], 0.0, 0.5, ALU.is_ge, ALU.subtract))
                step(dve.scalar_tensor_tensor(out=rfull[:, :], in0=src[:, :], scalar=4.0, in1=dst, op0=ALU.mult, op1=ALU.mult))
                dve.scalar_tensor_tensor(out=dst, in0=rfull[:, :], scalar=2.0 * GATE_MIN, in1=dst, op0=ALU.max,
                                         op1=ALU.mult).then_inc(gate_ready, 1)

            def sig_q(u):
                b, h = divmod(u, HEADS)
                dve.wait_ge(e_ready, u + 1)
                dve.scalar_tensor_tensor(out=sig[b][:, h, :], in0=ps_main[u % 2][:, :], scalar=bqs[:, 1, h:h + 1],
                                         in1=et[:, u % 2, :], op0=ALU.add, op1=ALU.max).then_inc(sig_ready, 1)

            def recip(b):
                dve.wait_ge(den_done, 2 * b + 2)
                step(dve.tensor_scalar(rfull[:, :], ps_den[:, :], EPS_DEN, None, ALU.add))
                step(dve.reciprocal(rfull[:, :], rfull[:, :]))
                if b == 1:
                    dve.wait_ge(bc_done, HEADS)
                step(dve.tensor_scalar(rrow[:, :], rfull[:, :], 1.0, None, ALU.mult))
                dve.scalar_tensor_tensor(out=rrow[:, :], in0=rrow[:, :].bitcast(F32), scalar=msk[:, 0:1], in1=rfull[:, :],
                                         op0=ALU.mult, op1=ALU.add).then_inc(rrow_ready, 1)

            def q_norm(n):
                b, h = divmod(n, HEADS)
                dve.wait_ge(bc_done, n + 1)
                dve.tensor_tensor(sig[b][:, h, :], sig[b][:, h, :], ps_bc[n % 2][:, :], ALU.mult).then_inc(qn_ready, 1)

            def q_lo(n):
                b, h = divmod(n, HEADS)
                dve.wait_ge(qh_pool if h % 2 else qh_act, n // 2 + 1)
                dve.tensor_tensor(ql[b][:, h, :], sig[b][:, h, :], qhi[b][:, h, :].bitcast(F32), ALU.subtract).then_inc(ql_ready, 1)

            def wo_sum(h):
                dve.wait_ge(woa_ready, h + 1)
                w = ring[:, slot(f"wo{h}"), :]
                dve.tensor_tensor(w[:, 0:HID], w[:, 0:HID], w[:, HID:2 * HID], ALU.add).then_inc(wos_ready, 1)

            def mw_lo(h):
                dve.wait_ge(mwh_ready, h + 1)
                dve.tensor_tensor(MW[:, 1, h, :], ps_t[h % 2][:, :], MW[:, 0, h, :].bitcast(F32), ALU.subtract).then_inc(mwl_ready, 1)

            for t in range(TPB):
                dve.wait_ge(x_in[t], 16)
                stats(t, 0, t)
            var_eps(TPB, 0, 0, TPB)
            rsqrt_finish(0, 0, 0, TPB)
            apply(0, 0, 0)
            apply(1, 0, 1)
            mod_finish(0, 0)
            mod_finish(1, 1)
            for t in range(2, TPB):
                apply(t, 0, t)
                ln1_lo(t - 2)
            ln1_lo(TPB - 2)
            wq_lo(0)
            ln1_lo(TPB - 1)
            wq_lo(1)
            dve.wait_ge(const, 3)
            idq = ident[:, :].rearrange("p (j i) -> p j i", j=4)
            for a in range(2):
                step(dve.tensor_tensor(pick[:, 4 * a:4 * a + 4], idq[:, :, a], idq[:, :, a + 2], ALU.add))
            step(dve.tensor_reduce(msk[:, 2:3], idq[:, :, 2:4], AX.XY, ALU.add))
            step(dve.tensor_scalar(msk[:, 0:1], msk[:, 2:3], -1.0, None, ALU.mult))
            step(dve.tensor_scalar(msk[:, 1:2], ident[:, 32:33], -1.0, None, ALU.mult))
            for b in range(B):
                step(dve.tensor_reduce(msk[:, 4 + b:5 + b], idq[:, :, b], AX.X, ALU.add))
            step(dve.tensor_tensor(pick_b[:, 0:1], ident[:, 0:1], ident[:, 32:33], ALU.add))
            dve.wait_ge(bias_in, 64)
            step(dve.tensor_scalar(brow[:, :], braw, 1.0, None, ALU.mult))
            dve.scalar_tensor_tensor(out=brow[:, :], in0=brow[:, :].bitcast(F32), scalar=msk[:, 1:2], in1=braw,
                                     op0=ALU.mult, op1=ALU.add).then_inc(mask_ready, 1)
            dve.wait_ge(bq_in, 16)
            step(dve.tensor_scalar(bqs[:, 1, :], bqs[:, 0, :], 1.0, None, ALU.add))
            dve.tensor_scalar(bqs[:, 2, :], bqs[:, 0, :], -1.0, None, ALU.mult).then_inc(bq_ready, 1)
            for t in range(TPB, TILES):
                dve.wait_ge(x_in[t], 16)
                stats(t, 0, t)
            var_eps(TILES, 0, TPB, TILES)
            rsqrt_finish(1, 0, TPB, TILES)
            apply(4, 0, 4)
            apply(5, 0, 5)
            wq_lo(2)
            for u in range(UNITS):
                if u + 3 < HEADS:
                    wq_lo(u + 3)
                sig_q(u)
                if u < 2:
                    ln1_lo(TPB + 2 * u)
                    ln1_lo(TPB + 2 * u + 1)
                if u == 0:
                    apply(6, 0, 6)
                    apply(7, 0, 7)
                if u == 3:
                    dve.wait_ge(z_in, 16)
                    dve.wait_ge(const, 4)
                    for a in range(2):
                        dve.tensor_copy(zcol[:, 4 * a:4 * a + 4, a::2],
                                        zin[:, 4 * a:4 * a + 4].unsqueeze(2).broadcast_to([P, 4, 16])).then_inc(zcol_ready, 1)
                    dve.wait_ge(map_in, 16)
                    step(dve.tensor_copy(mapf[:, :], mapi[:, :]))
                    for e in range(E):
                        step(dve.tensor_scalar(oneh[:, e, :], mapf[:, :], float(e), None, ALU.is_equal))
                if u in (4, 6):
                    gate_finish(u - 4)
                    gate_finish(u - 3)
                if u == 8:
                    mod_finish(2, 2)
                if u >= 9:
                    wo_sum(u - 9)
                if u == 10:
                    mod_finish(3, 3)
                    recip(0)
                if u >= 11:
                    mw_lo(u - 11)
                if u >= 12:
                    n = 2 * (u - 12)
                    q_norm(n)
                    q_norm(n + 1)
                    q_lo(n)
                    q_lo(n + 1)
            wo_sum(7)
            mw_lo(5)
            mw_lo(6)
            recip(1)
            mw_lo(7)
            for i in range(2):
                dve.wait_ge(fwh_ready, i + 1)
                raw = ring[:, slot(f"fw{i}"), 0:2 * FW].rearrange("p (k n) -> p k n", k=2)
                for k in range(2 * i, 2 * i + 2):
                    dve.tensor_tensor(flo(k)[:, 0:FW - 1], raw[:, k % 2, 0:FW - 1], fhi[:, k, 0:FW - 1].bitcast(F32),
                                      ALU.subtract).then_inc(fwl_ready, 1)
            dve.wait_ge(lbh_ready, 1)
            dve.tensor_tensor(lbs[1], ring[:, slot("lb"), 0:HID], lbs[0].bitcast(F32), ALU.subtract).then_inc(lbl_ready, 1)

            def attn_out(t):
                b = t // TPB
                dve.wait_ge(o_done, t + 1)
                dve.tensor_tensor(et[:, 0, :], ps_main[t % 2][:, :], gates[:, 0, b, :], ALU.mult).then_inc(og_ready, 1)
                dve.wait_ge(og_ready, t + 1)
                dve.tensor_tensor(x_sb[:, t, :], et[:, 0, :], x_sb[:, t, :], ALU.add).then_inc(x2_ready, 1)
                dve.wait_ge(x2_ready, t + 1)

            def route_max(t):
                dve.wait_ge(f_done, t + 1)
                dve.tensor_reduce(sms[:, t % 2, 0, 0:1], ps_ffn[t % 2][1][:, FB + ER:FB + ER + NR], AX.X, ALU.max,
                                  negate=True).then_inc(rmax_ready, 1)

            def route_weights(t):
                ex, rest, top = (sm[:, t % 2, i, 0:NR] for i in range(3))
                top8, w8, w8s = (sms[:, t % 2, i, :] for i in (1, 2, 3))
                dve.wait_ge(rexp_ready, t + 1)
                step(dve.reciprocal(sms[:, t % 2, 0, 2:3], sms[:, t % 2, 0, 1:2]))
                step(dve.max(top8, ex))
                step(dve.match_replace(rest, top8, ex, 0.0))
                step(dve.tensor_tensor(top, ex, rest, ALU.subtract))
                step(dve.tensor_tensor(wt[:, :, :], oneh[:, :, :], top.unsqueeze(1).broadcast_to([P, E, NR]), ALU.mult))
                step(dve.tensor_reduce(w8, wt[:, :, :], AX.X, ALU.add))
                step(dve.tensor_scalar(w8s, w8, sms[:, t % 2, 0, 2:3], SCALING, ALU.mult, ALU.mult))
                if t >= 1:
                    dve.wait_ge(hwT_done, t)
                dve.tensor_tensor(hw.rearrange("p (e r) -> p e r", e=E),
                                  ps_ffn[t % 2][1][:, FB:FB + ER].rearrange("p (e r) -> p e r", e=E),
                                  w8s.unsqueeze(2).broadcast_to([P, E, R]), ALU.mult).then_inc(hw_ready, 1)

            def hw_lo(t):
                dve.wait_ge(hwh_ready, t + 1)
                dve.tensor_tensor(hwT[:, 1, :], ps_mod[:, 0:P], hwT[:, 0, :].bitcast(F32), ALU.subtract).then_inc(hwl_ready, 1)

            def ffn_out(t):
                b = t // TPB
                dve.wait_ge(l_done, t + 1)
                dve.tensor_tensor(et[:, 1, 0:FH], ps_ffn[t % 2][0][:, 0:FH], gates[:, 1, b, 0:FH], ALU.mult).then_inc(fg_ready, 1)
                dve.tensor_tensor(et[:, 1, FH:HID], ps_ffn[t % 2][1][:, 0:FB], gates[:, 1, b, FH:HID], ALU.mult).then_inc(fg_ready, 1)
                dve.wait_ge(fg_ready, 2 * t + 2)
                dve.tensor_tensor(x_sb[:, t, :], et[:, 1, :], x_sb[:, t, :], ALU.add).then_inc(res_ready, 1)

            for s in range(TILES + 3):
                if s in (1, 2):
                    for n in (4 + 4 * s, 6 + 4 * s):
                        q_norm(n)
                        q_norm(n + 1)
                        q_lo(n)
                        q_lo(n + 1)
                if s < TILES:
                    attn_out(s)
                    stats(TILES + s, 1, s)
                    var_eps(TILES + s + 1, 1, s, s + 1)
                if 0 <= s - 3 < TILES:
                    hw_lo(s - 3)
                if s < TILES:
                    rsqrt_finish(2 + s, 1, s, s + 1)
                    apply(TILES + s, 1, s)
                if 0 <= s - 1 < TILES:
                    split_lo(TILES + s - 1, [h2[:, (s - 1) % 2, l, :, :] for l in range(2)])
                if 0 <= s - 2 < TILES:
                    route_max(s - 2)
                if 0 <= s - 3 < TILES:
                    ffn_out(s - 3)
                if 0 <= s - 2 < TILES:
                    route_weights(s - 2)

        @block.tensor
        def _(pe):
            def mod_rows(i):
                landed(pe, f"mod{i}")
                if i == 0:
                    pe.wait_ge(silu_ready, 1)
                else:
                    pe.wait_ge(mods_ready, [0, 1, 2, 2, 2, 3][i])
                    pe.wait_ge(gate_ready, [0, 0, 0, 2, 4, 4][i])
                w = ring[:, slot(f"mod{i}"), :].rearrange("p (k n) -> p k n", k=KC)
                for k in range(KC):
                    ins = pe.matmul(ps_mod[32 * k:32 * k + 32, :], sct[:, k, :], w[:, k, :], start=True, stop=True,
                                    skip_group_check=True)
                ins.then_inc(mod_done, 1)

            def mod_transpose(i):
                pe.wait_ge(mrow_ready, i + 1)
                if i == 0:
                    pe.wait_ge(const, 3)
                for k in range(KC):
                    ins = pe.transpose(ps_mod[:, k * P:(k + 1) * P], mrow[:, k * P:(k + 1) * P], ident[:, :])
                ins.then_inc(modT_done, 1)

            def gate_rows(n, i):
                pe.wait_ge(mrow_ready, i + 1)
                if n == 0:
                    pe.wait_ge(mask_ready, 1)
                if n == 2:
                    pe.wait_ge(gate_ready, 1)
                b = n % 2
                dst = ps_den if n % 2 == 0 else ps_mod
                pe.matmul(dst[:, :], msk[:, 4 + b:5 + b].broadcast_to([P, P]), mrow[:, :], start=True,
                          stop=True).then_inc(gate_done, 1)

            def transpose_tile(n, dst):
                pe.wait_ge(hn_ready, n + 1)
                for k in range(KC):
                    ins = pe.transpose(dst[:, k * P:(k + 1) * P], hn[:, n % 2, k * P:(k + 1) * P], ident[:, :])
                ins.then_inc(t_done, 1)

            def ln1_transpose(t):
                if t >= 2:
                    pe.wait_ge(full_ready, t - 1)
                transpose_tile(t, ps_t[t % 2])

            def query(u):
                b, h = divmod(u, HEADS)
                if h == 0:
                    pe.wait_ge(lo_ready, TPB * (b + 1))
                if b == 0:
                    pe.wait_ge(wql_ready, h + 1)
                if u >= 2:
                    pe.wait_ge(sig_ready, u - 1)
                n = 0
                for k in range(KC):
                    for w, a in ((0, 0), (0, 1), (1, 0)):
                        ins = pe.matmul(ps_main[u % 2][:, :], WQ[:, w, h, k, :], HT[:, b, a, k, :],
                                        start=(n == 0), stop=(n == 3 * KC - 1))
                        n += 1
                ins.then_inc(q_done, 1)

            def den(b, a):
                pe.wait_ge(sig_ready, HEADS * b + 4 * a + 4)
                if a == 0:
                    if b == 0:
                        pe.wait_ge(zcol_ready, 2)
                        pe.wait_ge(gate_ready, 3)
                    else:
                        pe.wait_ge(rrow_ready, 1)
                for j in range(4):
                    ins = pe.matmul(ps_den[32 * j:32 * j + 32, :], zcol[:, 4 * a + j, :], sig[b][:, 4 * a + j, :],
                                    start=(a == 0), stop=(a == 1), skip_group_check=True)
                ins.then_inc(den_done, 1)

            def spread(n):
                b, h = divmod(n, HEADS)
                if h == 0:
                    pe.wait_ge(rrow_ready, b + 1)
                if n >= 2:
                    pe.wait_ge(qn_ready, n - 1)
                pe.matmul(ps_bc[n % 2][:, :], pick[:, h:h + 1].broadcast_to([P, P]), rrow[:, :], start=True,
                          stop=True).then_inc(bc_done, 1)

            def fold(h):
                pe.wait_ge(wos_ready, h + 1)
                if h == 0:
                    pe.wait_ge(m_in, 16)
                    pe.wait_ge(full_ready, TILES)
                if h >= 2:
                    pe.wait_ge(mwl_ready, h - 1)
                pe.matmul(ps_t[h % 2][:, :], mT[:, h, :], ring[:, slot(f"wo{h}"), 0:HID], start=True,
                          stop=True).then_inc(mw_done, 1)

            def project(t, heads):
                b, tt = divmod(t, TPB)
                if heads[0] == 0:
                    if t == 0:
                        pe.wait_ge(mwl_ready, HEADS)
                        pe.wait_ge(sig_ready, UNITS)
                    if t >= 2:
                        pe.wait_ge(og_ready, t - 1)
                    pe.wait_ge(ql_ready, HEADS * (b + 1))
                cols = slice(tt * P, (tt + 1) * P)
                for h in heads:
                    for a, w in ((0, 0), (0, 1), (1, 0)):
                        lhs = (qhi if a == 0 else ql)[b][:, h, cols]
                        ins = pe.matmul(ps_main[t % 2][:, :], lhs, MW[:, w, h, :],
                                        start=(h == 0 and a == 0 and w == 0), stop=(h == HEADS - 1 and a == 1))
                if heads[-1] == HEADS - 1:
                    ins.then_inc(o_done, 1)

            def ffn(t):
                pe.wait_ge(lo_ready, TILES + t + 1)
                if t == 0:
                    pe.wait_ge(fwl_ready, KC)
                    pe.wait_ge(const, 8)
                if t == 1:
                    pe.wait_ge(qn_ready, UNITS)
                if t >= 2:
                    pe.wait_ge(fg_ready, 2 * (t - 1))
                for half in range(2):
                    dst = ps_ffn[t % 2][half][:, 0:FH]
                    cols = slice(half * FH, (half + 1) * FH)
                    pe.matmul(dst, pick_b[:, 0:1].broadcast_to([P, P]), brow[:, cols], start=True, stop=False)
                    for k in range(KC):
                        pe.matmul(dst, h2[:, t % 2, 0, k, :], fhi[:, k, cols], start=False, stop=False)
                        pe.matmul(dst, h2[:, t % 2, 0, k, :], flo(k)[:, cols], start=False, stop=False)
                        ins = pe.matmul(dst, h2[:, t % 2, 1, k, :], fhi[:, k, cols], start=False, stop=(k == KC - 1))
                ins.then_inc(f_done, 1)

            def hw_transpose(t):
                pe.wait_ge(hw_ready, t + 1)
                if t >= 1:
                    pe.wait_ge(hwl_ready, t)
                pe.transpose(ps_mod[:, 0:P], hw, ident[:, :]).then_inc(hwT_done, 1)

            def lora(t):
                pe.wait_ge(hwl_ready, t + 1)
                if t == 0:
                    pe.wait_ge(lbl_ready, 1)
                for dst, cols in ((ps_ffn[t % 2][0][:, 0:FH], slice(0, FH)), (ps_ffn[t % 2][1][:, 0:FB], slice(FH, HID))):
                    for a, w in ((0, 0), (0, 1), (1, 0)):
                        ins = pe.matmul(dst, hwT[:, a, :], lbs[w][:, cols], start=False, stop=True, skip_group_check=True)
                ins.then_inc(l_done, 1)

            mod_rows(0)
            mod_transpose(0)
            mod_rows(1)
            mod_transpose(1)
            for t in range(TPB):
                ln1_transpose(t)
            for u in range(UNITS):
                query(u)
                if u < 2:
                    ln1_transpose(TPB + 2 * u)
                    ln1_transpose(TPB + 2 * u + 1)
                if u in (2, 4):
                    mod_rows(2 + (u - 2) // 2)
                if u in (3, 5):
                    gate_rows(u - 3, 2 + (u - 3) // 2)
                    gate_rows(u - 2, 2 + (u - 3) // 2)
                if u in (6, 8):
                    mod_rows(4 + (u - 6) // 2)
                if u in (7, 9):
                    mod_transpose(4 + (u - 7) // 2)
                    den(0, (u - 7) // 2)
                if u >= 10:
                    fold(u - 10)
                if 11 <= u < 15:
                    spread(2 * (u - 11))
                    spread(2 * (u - 11) + 1)
                if u == 13:
                    den(1, 0)
            fold(6)
            den(1, 1)
            fold(7)
            first, last = range(0, HEADS // 2), range(HEADS // 2, HEADS)
            for s in range(TILES + 3):
                if s < TILES:
                    project(s, first)
                    if s in (1, 2):
                        spread(6 + 4 * s)
                        spread(7 + 4 * s)
                    project(s, last)
                    if s < 2:
                        spread(8 + 4 * s)
                        spread(9 + 4 * s)
                if 0 <= s - 1 < TILES:
                    t = s - 1
                    if t == 0:
                        pe.wait_ge(rrow_ready, 2)
                    if t >= 1:
                        pe.wait_ge(full_ready, TILES + t)
                    transpose_tile(TILES + t, ps_den)
                if 0 <= s - 3 < TILES:
                    hw_transpose(s - 3)
                if 0 <= s - 2 < TILES:
                    ffn(s - 2)
                if 0 <= s - 3 < TILES:
                    lora(s - 3)


def kernel(**inputs):
    import numpy as np
    import concourse.bacc as bacc
    from concourse import mybir as _mybir
    from concourse.bass_utils import run_bass_kernel_spmd

    def arr(name):
        return np.asarray(inputs[name])

    heads = slice(0, None, G)
    dram = {
        "x": arr("L0_attn_hidden_states").reshape(TILES, P, HID),
        "c": arr("L0_c").reshape(B, KC, P).transpose(2, 1, 0),
        "wmod": arr("L0_wmod").reshape(KC, P, 6, HID).transpose(2, 1, 0, 3).reshape(6, P, KC * HID),
        "wq": arr("L0_attn_Wq").reshape(HEADS * G, D, KC, P)[heads].reshape(2, 4, D, KC, P)
        .transpose(0, 4, 1, 3, 2).reshape(2, P, 4 * KC * D),
        "bq": arr("L0_attn_bq").reshape(HEADS * G, D)[heads].T,
        "z": arr("L0_attn_z").T,
        "wo": arr("L0_attn_Wo").reshape(HID, HEADS, G, D).transpose(1, 3, 2, 0).reshape(HEADS, D, G * HID),
        "m": arr("L0_attn_M").transpose(2, 0, 1),
        "fw": np.concatenate([arr("L0_ffn_base_W"), arr("L0_ffn_A").reshape(ER, HID), arr("L0_ffn_router_W")], 0)
        .T.reshape(KC, P, FW - 1).transpose(1, 0, 2),
        "lb": arr("L0_ffn_B").transpose(0, 2, 1).reshape(ER, HID),
        "bb": arr("L0_ffn_base_b").reshape(1, HID),
        "rb": arr("L0_ffn_router_b").reshape(1, NR),
        "map": arr("L0_ffn_expert_map").reshape(1, NR),
    }
    nc = bacc.Bacc("TRN2", target_bir_lowering=False, num_devices=1)
    arrays, args = {}, []
    for name, a in dram.items():
        a = np.ascontiguousarray(a)
        arrays[f"{name}_dram"] = a
        args.append(nc.dram_tensor(f"{name}_dram", a.shape, _mybir.dt.from_np(a.dtype), kind="ExternalInput").ap())
    out = nc.dram_tensor("out_dram", (TILES, P, HID), _mybir.dt.float32, kind="ExternalOutput").ap()
    build(nc, *args, out)
    r = run_bass_kernel_spmd(nc, [arrays], core_ids=[0])
    return r.results[0]["out_dram"].reshape(B, S, HID)
```

```python
from contextlib import ExitStack

import concourse.bass as bass
from concourse import mybir

F32 = mybir.dt.float32
F32R = mybir.dt.float32r
I32 = mybir.dt.int32
ALU = mybir.AluOpType
ACT = mybir.ActivationFunctionType
AX = mybir.AxisListType

P = 128
B, S, HID = 2, 512, 512
HEADS, D = 8, 128
G = 4
KC = HID // P
TILES = B * S // P
TPB = TILES // B
UNITS = B * HEADS
E, R = 8, 16
NR = 2 * E - 1
ER = E * R
FW = HID + ER + NR + 1
FH = FW // 2
FB = HID - FH
EPS_DEN = 1e-6
EPS_LN = 1e-5
GATE_MIN = 0.25
SCALING = 2.0
RING = 3
SLOT = G * HID
MODS = [("sa", 0), ("ca", 1), ("ga", 2), ("sb", 3), ("cb", 4), ("gb", 5)]
ITEMS = ["mod0", "mod1", "wq0", "wq1", "mod2"] + [f"wo{h}" for h in range(HEADS)] \
    + ["mod3", "mod4", "fw0", "fw1", "lb", "mod5"]


def build(nc, x_d, c_d, wmod_d, wq_d, bq_d, z_d, wo_d, m_d, fw_d, lb_d, bb_d, rb_d, map_d, out_d):
    with ExitStack() as ctx:
        def sb(name, shape, dt=F32):
            return ctx.enter_context(nc.sbuf_tensor(name, shape, dt))

        def sem(name):
            return ctx.enter_context(nc.semaphore(name))

        x_sb = sb("x_sb", [P, TILES, HID])
        hn = sb("hn", [P, 2, HID])
        hfull = sb("hfull", [P, 2, HID])
        HT = sb("HT", [P, B, 2, KC, S], F32R)
        WQ = sb("WQ", [P, 2, HEADS, KC, D], F32R)
        sig, ql = [], []
        for b in range(B):
            at = nc.sbuf_base
            sig.append(sb(f"sig{b}", [P, HEADS, S]))
            ql.append(nc.alloc_sbuf_tensor_at(f"ql{b}", [P, HEADS, S], F32R, offset=at))
        MW = sb("MW", [P, 2, HEADS, HID], F32R)
        ring = sb("ring", [P, RING, SLOT])
        mT = sb("mT", [P, HEADS, D])
        lb_hi = sb("lb_hi", [P, HID], F32R)
        ident = sb("ident", [P, P])
        zcol = sb("zcol", [P, HEADS, 32])
        rfull = sb("rfull", [P, S])
        rrow = sb("rrow", [P, S], F32R)
        gates = sb("gates", [P, 2, B, HID])
        mrow = sb("mrow", [P, HID])
        et = sb("et", [P, 2, S])
        brow = sb("brow", [P, FW], F32R)
        pick = sb("pick", [P, HEADS], F32R)
        pick_b = sb("pick_b", [P, 2], F32R)
        msk = sb("msk", [P, 8])
        sct = sb("sct", [P, KC, 32])
        cin = sb("cin", [P, KC, B])
        ce = sb("ce", [P, 3, KC, B])
        zin = sb("zin", [P, HEADS])
        bqs = sb("bqs", [P, 3, HEADS])
        mods = sb("mods", [P, 4, KC, B])
        stat = sb("stat", [P, TILES, 2, 6])
        mv = sb("mv", [P, 2, TILES, 2])
        rs = sb("rs", [P, 2, 6, TILES])
        mapi = sb("mapi", [P, NR], I32)
        mapf = sb("mapf", [P, NR])
        oneh = sb("oneh", [P, E, NR])
        sm = sb("sm", [P, 2, 4, 16])
        sms = sb("sms", [P, 2, 4, 8])
        wt = sb("wt", [P, E, NR])
        hw = rfull[:, 0:ER]
        hwT = rrow[:, 0:2 * P].rearrange("p (l t) -> p l t", l=2)
        HTf = HT[:, :, :, :, :].rearrange("p b l k s -> p b (l k s)")
        WQf = WQ[:, :, :, :, :].rearrange("p l h k d -> p (l h k d)")
        qhi = [HTf[:, 0, :].rearrange("p (h s) -> p h s", h=HEADS),
               WQf[:, 0:HEADS * S].rearrange("p (h s) -> p h s", h=HEADS)]
        h2 = HTf[:, 1, 0:2 * 2 * HID].rearrange("p (a l k t) -> p a l k t", a=2, l=2, k=KC)
        fhi = WQf[:, HEADS * S:HEADS * S + KC * FW].rearrange("p (k n) -> p k n", k=KC)
        flo3 = HTf[:, 1, 4 * HID:4 * HID + 3 * FW].rearrange("p (k n) -> p k n", k=3)
        flo1 = WQf[:, HEADS * S + KC * FW:HEADS * S + (KC + 1) * FW]
        lbs = [lb_hi[:, :], WQf[:, HEADS * S + (KC + 1) * FW:HEADS * S + (KC + 1) * FW + HID]]
        braw = gates[:, 0, :, :].rearrange("p b n -> p (b n)")[:, 0:FW]

        def flo(k):
            return flo3[:, k, :] if k < 3 else flo1

        bank = [ctx.enter_context(nc.psum_tensor(f"bank{i}", [P, 512], F32)) for i in range(8)]
        ps_main = [bank[0], bank[1]]
        ps_den = bank[2]
        ps_bc = [bank[3], bank[4]]
        ps_t = [bank[5], bank[6]]
        ps_h = bank[3:7]
        ps_mod = bank[7]
        ps_ffn = [[bank[5], bank[6]], [bank[3], bank[4]]]

        def mod_bank(i):
            return (ps_den if i == 1 else ps_mod)[:, :]

        def mod_row(i):
            return (rfull if i == 1 else mrow)[:, :]

        def gate_bank(n):
            return ps_den if n == 0 else ps_mod

        x_in = [sem(f"x_in{t}") for t in range(TILES)]
        ring_in = [sem(f"ring_in{s}") for s in range(RING)]
        c_in, z_in, bq_in, m_in, map_in = sem("c_in"), sem("z_in"), sem("bq_in"), sem("m_in"), sem("map_in")
        bias_in = sem("bias_in")
        const = sem("const")
        ec_ready, silu_ready = sem("ec_ready"), sem("silu_ready")
        setup = sem("setup")
        mask_ready, zcol_ready, brow_ready = sem("mask_ready"), sem("zcol_ready"), sem("brow_ready")
        mod_done, mrow_ready, modT_done, mods_ready = sem("mod_done"), sem("mrow_ready"), sem("modT_done"), sem("mods_ready")
        gate_done, gate_ready = sem("gate_done"), sem("gate_ready")
        gate_tmp = sem("gate_tmp")
        st_ready, newton = sem("st_ready"), sem("newton")
        hn_ready, t_done, full_ready, hi_ready, lo_ready = sem("hn_ready"), sem("t_done"), sem("full_ready"), sem("hi_ready"), sem("lo_ready")
        wqh_ready, wql_ready = sem("wqh_ready"), sem("wql_ready")
        q_done, neg_ready, e_ready, bq_ready, sig_ready = sem("q_done"), sem("neg_ready"), sem("e_ready"), sem("bq_ready"), sem("sig_ready")
        den_done, r_ready, rrow_ready = sem("den_done"), sem("r_ready"), sem("rrow_ready")
        bc_done, qn_ready, qh_act, qh_pool, ql_ready = sem("bc_done"), sem("qn_ready"), sem("qh_act"), sem("qh_pool"), sem("ql_ready")
        woa_ready, wos_ready, mw_done, mwh_ready, mwl_ready = sem("woa_ready"), sem("wos_ready"), sem("mw_done"), sem("mwh_ready"), sem("mwl_ready")
        fwh_ready, fwl_ready, lbh_ready, lbl_ready = sem("fwh_ready"), sem("fwl_ready"), sem("lbh_ready"), sem("lbl_ready")
        o_done, og_ready, x2_ready = sem("o_done"), sem("og_ready"), sem("x2_ready")
        fr_done, f_done, rmax_ready, rexp_ready, route, hw_ready = sem("fr_done"), sem("f_done"), sem("rmax_ready"), sem("rexp_ready"), sem("route"), sem("hw_ready")
        hwT_done, hwh_ready, hwl_ready, l_done = sem("hwT_done"), sem("hwh_ready"), sem("hwl_ready"), sem("l_done")
        fg_ready, res_ready, out_in = sem("fg_ready"), sem("res_ready"), sem("out_in")
        block = ctx.enter_context(nc.Block())

        item = {name: i for i, name in enumerate(ITEMS)}

        def slot(name):
            return item[name] % RING

        def landed(eng, name):
            eng.wait_ge(ring_in[item[name] % RING], 16 * (item[name] // RING + 1))

        @block.sync
        def _(sp):
            def released(name):
                i = int(name[-1]) if name != "lb" else 0
                if name.startswith("mod"):
                    sp.wait_ge(mod_done, i + 1)
                elif name.startswith("wq"):
                    sp.wait_ge(wqh_ready, 4 * i + 4)
                    sp.wait_ge(wql_ready, 4 * i + 4)
                elif name.startswith("wo"):
                    sp.wait_ge(mw_done, i + 1)
                elif name.startswith("fw"):
                    sp.wait_ge(fwh_ready, i + 1)
                    sp.wait_ge(fwl_ready, 2 * i + 2)

            def load(name):
                n = item[name]
                if n >= RING:
                    released(ITEMS[n - RING])
                dst = ring[:, n % RING, :]
                i = int(name[-1]) if name != "lb" else 0
                if name.startswith("mod"):
                    src = wmod_d[MODS[i][1]]
                elif name.startswith("wq"):
                    src = wq_d[i]
                elif name.startswith("wo"):
                    src = wo_d[i]
                elif name.startswith("fw"):
                    dst = dst[:, 0:2 * FW].rearrange("p (k n) -> p k n", k=2)[:, :, 0:FW - 1]
                    src = fw_d[:, 2 * i:2 * i + 2, :]
                else:
                    dst, src = dst[:, 0:HID], lb_d
                sp.dma_start(dst, src).then_inc(ring_in[n % RING], 16)

            sp.dma_start(cin[:, :, :], c_d).then_inc(c_in, 16)
            for t in range(TPB):
                sp.dma_start(x_sb[:, t, :], x_d[t]).then_inc(x_in[t], 16)
            load("mod0")
            load("mod1")
            load("wq0")
            sp.dma_start(bqs[:, 0, :], bq_d).then_inc(bq_in, 16)
            sp.dma_start(zin[:, :], z_d).then_inc(z_in, 16)
            for t in range(TPB, TILES):
                sp.dma_start(x_sb[:, t, :], x_d[t]).then_inc(x_in[t], 16)
            load("wq1")
            sp.dma_start(mT[:, :, :], m_d).then_inc(m_in, 16)
            sp.dma_start(mapi[:, :], map_d.broadcast_to([P, NR])).then_inc(map_in, 16)
            for name in ITEMS[4:]:
                load(name)
            for t in range(TILES):
                sp.wait_ge(res_ready, t + 1)
                sp.dma_start(out_d[t], x_sb[:, t, :]).then_inc(out_in, 16)
            sp.wait_ge(out_in, 16 * TILES)

        @block.gpsimd
        def _(pool):
            pool.memset(sct[:, :, :], 0.0).then_inc(const, 1)
            pool.memset(ident[:, :], 0.0).then_inc(const, 1)
            pool.wait_ge(const, 2)
            pool.affine_select(out=ident[:, :], in_=ident[:, :], compare_op=ALU.not_equal, fill=1.0, base=0,
                               pattern=[[-1, P]], channel_multiplier=1).then_inc(const, 1)
            pool.memset(zcol[:, :, :], 0.0).then_inc(const, 1)
            pool.memset(braw, 0.0).then_inc(const, 1)
            pool.wait_ge(const, 5)
            for p in (0, 32):
                pool.dma_start(braw[p:p + 1, 0:HID], bb_d).then_inc(bias_in, 16)
                pool.dma_start(braw[p:p + 1, HID + ER:HID + ER + NR], rb_d).then_inc(bias_in, 16)

            def wq_hi(h):
                if h % 4 == 0:
                    landed(pool, f"wq{h // 4}")
                src = ring[:, slot(f"wq{h // 4}"), :].rearrange("p (h n) -> p h n", h=4)[:, h % 4, :]
                pool.tensor_scalar(WQ[:, 0, h, :, :].rearrange("p k d -> p (k d)"), src, 1.0, 1.0,
                                   ALU.mult, ALU.mult).then_inc(wqh_ready, 1)

            def q_hi(n):
                b, h = divmod(n, HEADS)
                if h == 1:
                    pool.wait_ge(q_done, HEADS * (b + 1))
                pool.wait_ge(qn_ready, n + 1)
                pool.tensor_scalar(qhi[b][:, h, :], sig[b][:, h, :], 1.0, 1.0, ALU.mult, ALU.mult).then_inc(qh_pool, 1)

            def wo_add(h):
                landed(pool, f"wo{h}")
                w = ring[:, slot(f"wo{h}"), :]
                pool.tensor_tensor(w[:, 0:2 * HID], w[:, 0:2 * HID], w[:, 2 * HID:4 * HID], ALU.add).then_inc(woa_ready, 1)

            for h in range(HEADS):
                wq_hi(h)
            for h in range(HEADS):
                wo_add(h)
            for n in range(1, HEADS, 2):
                q_hi(n)
            pool.wait_ge(q_done, UNITS)
            pool.memset(fhi[:, :, FW - 1:FW].bitcast(F32), 0.0).then_inc(const, 1)
            pool.memset(flo3[:, :, FW - 1:FW].bitcast(F32), 0.0).then_inc(const, 1)
            pool.memset(flo1[:, FW - 1:FW].bitcast(F32), 0.0).then_inc(const, 1)
            for i in range(2):
                landed(pool, f"fw{i}")
                src = ring[:, slot(f"fw{i}"), 0:2 * FW].rearrange("p (k n) -> p k n", k=2)[:, :, 0:FW - 1]
                pool.tensor_scalar(fhi[:, 2 * i:2 * i + 2, 0:FW - 1], src, 1.0, 1.0, ALU.mult, ALU.mult).then_inc(fwh_ready, 1)
            landed(pool, "lb")
            pool.tensor_scalar(lbs[0], ring[:, slot("lb"), 0:HID], 1.0, 1.0, ALU.mult, ALU.mult).then_inc(lbh_ready, 1)
            for n in range(HEADS + 1, UNITS, 2):
                q_hi(n)

        @block.scalar
        def _(act):
            act.wait_ge(c_in, 16)
            act.activation(ce[:, 0, :, :], cin[:, :, :], ACT.Exp, scale=-1.0).then_inc(ec_ready, 1)

            def mod_evac(i):
                act.wait_ge(mod_done, i + 1)
                if i in (2, 4, 5):
                    act.wait_ge(modT_done, {2: 1, 4: 3, 5: 4}[i])
                if i == 3:
                    act.wait_ge(gate_done, B)
                act.activation(mod_row(i), mod_bank(i), ACT.Copy).then_inc(mrow_ready, 1)

            def modulate(n, layer, b, k, dst, src):
                return act.activation(dst, src, ACT.Identity, bias=mods[:, 2 * layer, k, b:b + 1],
                                      scale=mods[:, 2 * layer + 1, k, b:b + 1])

            def ln1_chunk(n):
                b, k = divmod(n, KC)
                act.wait_ge(t_done, TPB * (b + 1))
                act.wait_ge(mods_ready, 2)
                if n >= 2:
                    act.wait_ge(lo_ready, n - 1)
                modulate(n, 0, b, k, hfull[:, n % 2, :], ps_h[k][:, :]).then_inc(full_ready, 1)
                act.wait_ge(full_ready, n + 1)
                act.activation(HT[:, b, 0, k, :], hfull[:, n % 2, :], ACT.Copy).then_inc(hi_ready, 1)

            def ln2_tile(t):
                n = TILES + t
                act.wait_ge(t_done, n + 1)
                act.wait_ge(mods_ready, 4)
                act.wait_ge(lo_ready, n - 1)
                if t >= 2:
                    act.wait_ge(f_done, t - 1)
                for k in range(KC):
                    ins = modulate(n, 1, t // TPB, k, hfull[:, n % 2, k * P:(k + 1) * P], ps_den[:, k * P:(k + 1) * P])
                ins.then_inc(full_ready, 1)
                act.wait_ge(full_ready, n + 1)
                act.activation(h2[:, t % 2, 0, :, :].rearrange("p k t -> p (k t)"), hfull[:, n % 2, :],
                               ACT.Copy).then_inc(hi_ready, 1)

            def exp_q(u):
                act.wait_ge(q_done, u + 1)
                if u == 0:
                    act.wait_ge(bq_ready, 1)
                if u >= 2:
                    act.wait_ge(sig_ready, u - 1)
                h = u % HEADS
                act.activation(et[:, u % 2, :], ps_main[u % 2][:, :], ACT.Relu, bias=bqs[:, 2, h:h + 1], scale=-1.0).then_inc(neg_ready, 1)
                act.wait_ge(neg_ready, u + 1)
                act.activation(et[:, u % 2, :], et[:, u % 2, :], ACT.Exp, scale=-1.0).then_inc(e_ready, 1)

            def q_hi(n):
                b, h = divmod(n, HEADS)
                if h == 0:
                    act.wait_ge(q_done, HEADS * (b + 1))
                act.wait_ge(qn_ready, n + 1)
                act.activation(qhi[b][:, h, :], sig[b][:, h, :], ACT.Copy).then_inc(qh_act, 1)

            def mw_hi(h):
                act.wait_ge(mw_done, h + 1)
                act.activation(MW[:, 0, h, :], ps_t[h % 2][:, :], ACT.Copy).then_inc(mwh_ready, 1)

            mod_evac(0)
            mod_evac(1)
            for n in range(KC):
                ln1_chunk(n)
            for u in range(UNITS):
                if u == 3:
                    mod_evac(2)
                if 6 <= u < 14:
                    mw_hi(u - 6)
                if u in (13, 15):
                    mod_evac(3 + (u - 13) // 2)
                exp_q(u)
                if u in (2, 3):
                    ln1_chunk(2 * u)
                    ln1_chunk(2 * u + 1)
                if u >= 12:
                    q_hi(2 * (u - 12))

            for s in range(TILES + 3):
                if s in (1, 2):
                    q_hi(4 + 4 * s)
                    q_hi(6 + 4 * s)
                if 0 <= s - 3 < TILES:
                    act.wait_ge(hwT_done, s - 2)
                    if s - 3 >= 1:
                        act.wait_ge(l_done, s - 3)
                    act.activation(hwT[:, 0, :], ps_mod[:, 0:P], ACT.Copy).then_inc(hwh_ready, 1)
                if s == 1:
                    mod_evac(5)
                if 0 <= s - 1 < TILES:
                    ln2_tile(s - 1)
                if 0 <= s - 2 < TILES:
                    t = s - 2
                    act.wait_ge(rmax_ready, t + 1)
                    act.activation(sm[:, t % 2, 0, 0:NR], ps_ffn[t % 2][1][:, FB + ER:FB + ER + NR], ACT.Exp,
                                   bias=sms[:, t % 2, 0, 0:1], accum_out=sms[:, t % 2, 0, 1:2]).then_inc(rexp_ready, 1)

        @block.vector
        def _(dve):
            steps = [0]

            def step(ins):
                steps[0] += 1
                ins.then_inc(setup, 1)
                dve.wait_ge(setup, steps[0])

            dve.wait_ge(ec_ready, 1)
            step(dve.tensor_scalar(ce[:, 1, :, :], ce[:, 0, :, :], 1.0, None, ALU.add))
            step(dve.reciprocal(ce[:, 2, :, :], ce[:, 1, :, :]))
            dve.wait_ge(const, 1)
            dve.tensor_tensor(sct[:, :, 0:B], cin[:, :, :], ce[:, 2, :, :], ALU.mult).then_inc(silu_ready, 1)

            def stats(n, layer, t):
                dve.bn_stats(stat[:, t, layer, :], x_sb[:, t, :]).then_inc(st_ready, 1)
                dve.wait_ge(st_ready, 2 * n + 1)
                dve.bn_aggr(mv[:, layer, t, :], stat[:, t, layer, :]).then_inc(st_ready, 1)

            def rsqrt(n, layer, lo, hi):
                v, hv, y, t = (rs[:, layer, i, lo:hi] for i in (0, 1, 2, 3))
                step(dve.tensor_scalar(v, mv[:, layer, lo:hi, 1], EPS_LN, None, ALU.add))
                step(dve.tensor_scalar(hv, v, -0.5, None, ALU.mult))
                step(dve.tensor_scalar(t.bitcast(I32), v.bitcast(I32), 1, None, ALU.logical_shift_right))
                step(dve.tensor_scalar(y.bitcast(I32), t.bitcast(I32), -1.0, float(0x5F3759DF), ALU.mult, ALU.add))
                for i in range(3):
                    if hi - lo == 1:
                        step(dve.scalar_tensor_tensor(out=t, in0=y, scalar=hv, in1=y, op0=ALU.mult, op1=ALU.mult))
                    else:
                        step(dve.tensor_tensor(t, y, y, ALU.mult))
                        step(dve.tensor_tensor(t, t, hv, ALU.mult))
                    ins = dve.scalar_tensor_tensor(out=y, in0=t, scalar=1.5, in1=y, op0=ALU.add, op1=ALU.mult)
                    if i < 2:
                        step(ins)
                ins.then_inc(newton, 1)
                dve.wait_ge(newton, n + 1)

            def apply(n, layer, t):
                if n >= 2:
                    dve.wait_ge(t_done, n - 1)
                dve.tensor_scalar(hn[:, n % 2, :], x_sb[:, t, :], mv[:, layer, t, 0:1], rs[:, layer, 2, t:t + 1],
                                  ALU.subtract, ALU.mult).then_inc(hn_ready, 1)

            def split_lo(n, dst):
                dve.wait_ge(hi_ready, n + 1)
                dve.tensor_tensor(dst[1], hfull[:, n % 2, :], dst[0].bitcast(F32), ALU.subtract).then_inc(lo_ready, 1)

            def ln1_lo(n):
                split_lo(n, [HT[:, n // KC, l, n % KC, :] for l in range(2)])

            def wq_lo(h):
                dve.wait_ge(wqh_ready, h + 1)
                src = ring[:, slot(f"wq{h // 4}"), :].rearrange("p (h n) -> p h n", h=4)[:, h % 4, :]
                hi, lo = (WQ[:, l, h, :, :].rearrange("p k d -> p (k d)") for l in range(2))
                dve.tensor_tensor(lo, src, hi.bitcast(F32), ALU.subtract).then_inc(wql_ready, 1)

            def mod_finish(i, n):
                dve.wait_ge(modT_done, n + 1)
                src = mod_bank([0, 1, 3, 4][i]).rearrange("p (k q r) -> p k r q", k=KC, q=4)[:, :, 0:B, :]
                dst = mods[:, i, :, :]
                if i % 2 == 0:
                    dve.tensor_reduce(dst, src, AX.X, ALU.add).then_inc(mods_ready, 1)
                else:
                    step(dve.tensor_reduce(dst, src, AX.X, ALU.add))
                    dve.tensor_scalar(dst, dst, 1.0, None, ALU.add).then_inc(mods_ready, 1)

            def gate_finish(n):
                dve.wait_ge(gate_done, n + 1)
                src = gate_bank(n)
                g, b = divmod(n, 2)
                dst = gates[:, g, b, :]
                tmp = et[:, 1, :] if g else rfull[:, :]
                step(dve.tensor_scalar(dst, src[:, :], 0.0, 0.5, ALU.is_ge, ALU.subtract))
                step(dve.scalar_tensor_tensor(out=tmp, in0=src[:, :], scalar=4.0, in1=dst, op0=ALU.mult, op1=ALU.mult))
                dve.scalar_tensor_tensor(out=dst, in0=tmp, scalar=2.0 * GATE_MIN, in1=dst, op0=ALU.max,
                                         op1=ALU.mult).then_inc(gate_ready, 1)

            def sig_q(u):
                b, h = divmod(u, HEADS)
                dve.wait_ge(e_ready, u + 1)
                dve.scalar_tensor_tensor(out=sig[b][:, h, :], in0=ps_main[u % 2][:, :], scalar=bqs[:, 1, h:h + 1],
                                         in1=et[:, u % 2, :], op0=ALU.add, op1=ALU.max).then_inc(sig_ready, 1)

            def recip(b, half):
                cols = slice(half * S // 2, (half + 1) * S // 2)
                dve.wait_ge(den_done, 2 * b + 2)
                step(dve.tensor_scalar(rfull[:, cols], ps_den[:, cols], EPS_DEN, None, ALU.add))
                step(dve.reciprocal(rfull[:, cols], rfull[:, cols]))
                if half == 1:
                    if b == 1:
                        dve.wait_ge(bc_done, HEADS)
                    step(dve.tensor_scalar(rrow[:, :], rfull[:, :], 1.0, None, ALU.mult))
                    dve.scalar_tensor_tensor(out=rrow[:, :], in0=rrow[:, :].bitcast(F32), scalar=msk[:, 0:1],
                                             in1=rfull[:, :], op0=ALU.mult, op1=ALU.add).then_inc(rrow_ready, 1)

            def q_norm(n):
                b, h = divmod(n, HEADS)
                dve.wait_ge(bc_done, n + 1)
                dve.tensor_tensor(sig[b][:, h, :], sig[b][:, h, :], ps_bc[n % 2][:, :], ALU.mult).then_inc(qn_ready, 1)

            def q_lo(n):
                b, h = divmod(n, HEADS)
                dve.wait_ge(qh_pool if h % 2 else qh_act, n // 2 + 1)
                dve.tensor_tensor(ql[b][:, h, :], sig[b][:, h, :], qhi[b][:, h, :].bitcast(F32), ALU.subtract).then_inc(ql_ready, 1)

            def wo_sum(h):
                dve.wait_ge(woa_ready, h + 1)
                w = ring[:, slot(f"wo{h}"), :]
                dve.tensor_tensor(w[:, 0:HID], w[:, 0:HID], w[:, HID:2 * HID], ALU.add).then_inc(wos_ready, 1)

            def mw_lo(h):
                dve.wait_ge(mwh_ready, h + 1)
                dve.tensor_tensor(MW[:, 1, h, :], ps_t[h % 2][:, :], MW[:, 0, h, :].bitcast(F32), ALU.subtract).then_inc(mwl_ready, 1)

            for t in range(TPB):
                dve.wait_ge(x_in[t], 16)
                stats(t, 0, t)
            dve.wait_ge(st_ready, 2 * TPB)
            rsqrt(0, 0, 0, TPB)
            for t in range(TPB):
                apply(t, 0, t)
            dve.wait_ge(const, 3)
            idq = ident[:, :].rearrange("p (j i) -> p j i", j=4)
            for a in range(2):
                step(dve.tensor_tensor(pick[:, 4 * a:4 * a + 4], idq[:, :, a], idq[:, :, a + 2], ALU.add))
            step(dve.tensor_reduce(msk[:, 2:3], idq[:, :, 2:4], AX.XY, ALU.add))
            step(dve.tensor_scalar(msk[:, 0:1], msk[:, 2:3], -1.0, None, ALU.mult))
            step(dve.tensor_scalar(msk[:, 1:2], ident[:, 32:33], -1.0, None, ALU.mult))
            for b in range(B):
                step(dve.tensor_reduce(msk[:, 4 + b:5 + b], idq[:, :, b], AX.X, ALU.add))
            dve.tensor_tensor(pick_b[:, 0:1], ident[:, 0:1], ident[:, 32:33], ALU.add).then_inc(mask_ready, 1)
            mod_finish(0, 0)
            mod_finish(1, 1)
            wq_lo(0)
            for n in range(KC):
                ln1_lo(n)
            wq_lo(1)
            dve.wait_ge(bq_in, 16)
            step(dve.tensor_scalar(bqs[:, 1, :], bqs[:, 0, :], 1.0, None, ALU.add))
            dve.tensor_scalar(bqs[:, 2, :], bqs[:, 0, :], -1.0, None, ALU.mult).then_inc(bq_ready, 1)
            for t in range(TPB, TILES):
                dve.wait_ge(x_in[t], 16)
                stats(t, 0, t)
            wq_lo(2)
            for u in range(UNITS):
                if u == 0:
                    dve.wait_ge(st_ready, 2 * TILES)
                    rsqrt(1, 0, TPB, TILES)
                    apply(4, 0, 4)
                    apply(5, 0, 5)
                if u == 1:
                    apply(6, 0, 6)
                    apply(7, 0, 7)
                if u in (4, 5):
                    gate_finish(u - 4)
                if 5 <= u < 13:
                    wo_sum(u - 5)
                if u == 14:
                    mod_finish(2, 2)
                if u >= 12:
                    q_norm(2 * (u - 12))
                    q_norm(2 * (u - 12) + 1)
                sig_q(u)
                if u == 0:
                    wq_lo(3)
                if u in (1, 2):
                    wq_lo(2 + 2 * u)
                    wq_lo(3 + 2 * u)
                if u == 2:
                    dve.wait_ge(z_in, 16)
                    dve.wait_ge(const, 4)
                    for a in range(2):
                        dve.tensor_copy(zcol[:, 4 * a:4 * a + 4, a::2],
                                        zin[:, 4 * a:4 * a + 4].unsqueeze(2).broadcast_to([P, 4, 16])).then_inc(zcol_ready, 1)
                    dve.wait_ge(bias_in, 64)
                    step(dve.tensor_scalar(brow[:, :], braw, 1.0, None, ALU.mult))
                    dve.scalar_tensor_tensor(out=brow[:, :], in0=brow[:, :].bitcast(F32), scalar=msk[:, 1:2], in1=braw,
                                             op0=ALU.mult, op1=ALU.add).then_inc(brow_ready, 1)
                    dve.wait_ge(brow_ready, 1)
                if u in (2, 3):
                    ln1_lo(2 * u)
                    ln1_lo(2 * u + 1)
                if u == 7:
                    dve.wait_ge(map_in, 16)
                    step(dve.tensor_copy(mapf[:, :], mapi[:, :]))
                    for e in range(E):
                        step(dve.tensor_scalar(oneh[:, e, :], mapf[:, :], float(e), None, ALU.is_equal))
                if u in (9, 10):
                    recip(0, u - 9)
                if 6 <= u < 14:
                    mw_lo(u - 6)
                if u >= 13:
                    q_lo(2 * (u - 13))
                    q_lo(2 * (u - 13) + 1)
            q_lo(6)
            q_lo(7)
            mod_finish(3, 3)
            recip(1, 0)
            recip(1, 1)
            for i in range(2):
                dve.wait_ge(fwh_ready, i + 1)
                raw = ring[:, slot(f"fw{i}"), 0:2 * FW].rearrange("p (k n) -> p k n", k=2)
                for k in range(2 * i, 2 * i + 2):
                    dve.tensor_tensor(flo(k)[:, 0:FW - 1], raw[:, k % 2, 0:FW - 1], fhi[:, k, 0:FW - 1].bitcast(F32),
                                      ALU.subtract).then_inc(fwl_ready, 1)
            dve.wait_ge(lbh_ready, 1)
            dve.tensor_tensor(lbs[1], ring[:, slot("lb"), 0:HID], lbs[0].bitcast(F32), ALU.subtract).then_inc(lbl_ready, 1)

            def attn_out(t):
                b = t // TPB
                dve.wait_ge(o_done, t + 1)
                dve.tensor_tensor(et[:, 0, :], ps_main[t % 2][:, :], gates[:, 0, b, :], ALU.mult).then_inc(og_ready, 1)
                dve.wait_ge(og_ready, t + 1)
                dve.tensor_tensor(x_sb[:, t, :], et[:, 0, :], x_sb[:, t, :], ALU.add).then_inc(x2_ready, 1)
                dve.wait_ge(x2_ready, t + 1)

            def route_max(t):
                dve.wait_ge(fr_done, t + 1)
                dve.tensor_reduce(sms[:, t % 2, 0, 0:1], ps_ffn[t % 2][1][:, FB + ER:FB + ER + NR], AX.X, ALU.max,
                                  negate=True).then_inc(rmax_ready, 1)

            def route_weights(t):
                ex, rest, top = (sm[:, t % 2, i, 0:NR] for i in range(3))
                top8, w8, w8s = (sms[:, t % 2, i, :] for i in (1, 2, 3))
                dve.wait_ge(rexp_ready, t + 1)
                step(dve.reciprocal(sms[:, t % 2, 0, 2:3], sms[:, t % 2, 0, 1:2]))
                step(dve.max(top8, ex))
                step(dve.match_replace(rest, top8, ex, 0.0))
                step(dve.tensor_tensor(top, ex, rest, ALU.subtract))
                step(dve.tensor_tensor(wt[:, :, :], oneh[:, :, :], top.unsqueeze(1).broadcast_to([P, E, NR]), ALU.mult))
                step(dve.tensor_reduce(w8, wt[:, :, :], AX.X, ALU.add))
                step(dve.tensor_scalar(w8s, w8, sms[:, t % 2, 0, 2:3], SCALING, ALU.mult, ALU.mult))
                if t >= 1:
                    dve.wait_ge(hwT_done, t)
                dve.tensor_tensor(hw.rearrange("p (e r) -> p e r", e=E),
                                  ps_ffn[t % 2][1][:, FB:FB + ER].rearrange("p (e r) -> p e r", e=E),
                                  w8s.unsqueeze(2).broadcast_to([P, E, R]), ALU.mult).then_inc(hw_ready, 1)

            def hw_lo(t):
                dve.wait_ge(hwh_ready, t + 1)
                dve.tensor_tensor(hwT[:, 1, :], ps_mod[:, 0:P], hwT[:, 0, :].bitcast(F32), ALU.subtract).then_inc(hwl_ready, 1)

            def ffn_out(t):
                b = t // TPB
                dve.wait_ge(l_done, t + 1)
                dve.tensor_tensor(et[:, 1, 0:FH], ps_ffn[t % 2][0][:, 0:FH], gates[:, 1, b, 0:FH], ALU.mult).then_inc(fg_ready, 1)
                dve.tensor_tensor(et[:, 1, FH:HID], ps_ffn[t % 2][1][:, 0:FB], gates[:, 1, b, FH:HID], ALU.mult).then_inc(fg_ready, 1)
                dve.wait_ge(fg_ready, 2 * t + 2)
                dve.tensor_tensor(x_sb[:, t, :], et[:, 1, :], x_sb[:, t, :], ALU.add).then_inc(res_ready, 1)

            for s in range(TILES + 3):
                if s in (1, 2):
                    for n in (4 + 4 * s, 6 + 4 * s):
                        q_norm(n)
                        q_norm(n + 1)
                        q_lo(n)
                        q_lo(n + 1)
                if s < TILES:
                    attn_out(s)
                    stats(TILES + s, 1, s)
                    dve.wait_ge(st_ready, 2 * (TILES + s + 1))
                if 0 <= s - 3 < TILES:
                    hw_lo(s - 3)
                if s < TILES:
                    rsqrt(2 + s, 1, s, s + 1)
                    apply(TILES + s, 1, s)
                if 0 <= s - 1 < TILES:
                    split_lo(TILES + s - 1, [h2[:, (s - 1) % 2, l, :, :].rearrange("p k t -> p (k t)") for l in range(2)])
                if 0 <= s - 2 < TILES:
                    route_max(s - 2)
                if 0 <= s - 3 < TILES:
                    ffn_out(s - 3)
                if 0 <= s - 2 < TILES:
                    route_weights(s - 2)
                if s in (1, 2):
                    gate_finish(s + 1)

        @block.tensor
        def _(pe):
            def mod_rows(i):
                landed(pe, f"mod{i}")
                if i == 0:
                    pe.wait_ge(silu_ready, 1)
                if i in (2, 4, 5):
                    pe.wait_ge(mods_ready, {2: 1, 4: 3, 5: 4}[i])
                if i == 3:
                    pe.wait_ge(gate_ready, B)
                w = ring[:, slot(f"mod{i}"), :].rearrange("p (k n) -> p k n", k=KC)
                for k in range(KC):
                    ins = pe.matmul(mod_bank(i)[32 * k:32 * k + 32, :], sct[:, k, :], w[:, k, :], start=True, stop=True,
                                    skip_group_check=True)
                ins.then_inc(mod_done, 1)

            def mod_transpose(i):
                pe.wait_ge(mrow_ready, i + 1)
                for k in range(KC):
                    ins = pe.transpose(mod_bank(i)[:, k * P:(k + 1) * P], mod_row(i)[:, k * P:(k + 1) * P], ident[:, :])
                ins.then_inc(modT_done, 1)

            def gate_rows(n, i):
                pe.wait_ge(mrow_ready, i + 1)
                if n == 0:
                    pe.wait_ge(mask_ready, 1)
                    pe.wait_ge(mods_ready, 2)
                if n == 3:
                    pe.wait_ge(gate_ready, 3)
                b = n % 2
                pe.matmul(gate_bank(n)[:, :], msk[:, 4 + b:5 + b].broadcast_to([P, P]), mrow[:, :], start=True,
                          stop=True).then_inc(gate_done, 1)

            def ln1_transpose(t):
                pe.wait_ge(hn_ready, t + 1)
                if t >= TPB:
                    pe.wait_ge(full_ready, KC)
                if t == 0:
                    pe.wait_ge(const, 3)
                for k in range(KC):
                    ins = pe.transpose(ps_h[k][:, (t % TPB) * P:(t % TPB + 1) * P], hn[:, t % 2, k * P:(k + 1) * P],
                                       ident[:, :])
                ins.then_inc(t_done, 1)

            def ln2_transpose(t):
                pe.wait_ge(hn_ready, TILES + t + 1)
                if t == 0:
                    pe.wait_ge(rrow_ready, 2)
                else:
                    pe.wait_ge(full_ready, TILES + t)
                for k in range(KC):
                    ins = pe.transpose(ps_den[:, k * P:(k + 1) * P], hn[:, t % 2, k * P:(k + 1) * P], ident[:, :])
                ins.then_inc(t_done, 1)

            def query(u):
                b, h = divmod(u, HEADS)
                if b == 0:
                    pe.wait_ge(wql_ready, h + 1)
                if u >= 2:
                    pe.wait_ge(sig_ready, u - 1)
                n = 0
                for k in range(KC):
                    if h == 0:
                        pe.wait_ge(lo_ready, KC * b + k + 1)
                    for w, a in ((0, 0), (0, 1), (1, 0)):
                        ins = pe.matmul(ps_main[u % 2][:, :], WQ[:, w, h, k, :], HT[:, b, a, k, :],
                                        start=(n == 0), stop=(n == 3 * KC - 1))
                        n += 1
                ins.then_inc(q_done, 1)

            def den(b, a):
                pe.wait_ge(sig_ready, HEADS * b + 4 * a + 4)
                if a == 0:
                    if b == 0:
                        pe.wait_ge(zcol_ready, 2)
                        pe.wait_ge(gate_ready, 1)
                    else:
                        pe.wait_ge(rrow_ready, 1)
                for j in range(4):
                    ins = pe.matmul(ps_den[32 * j:32 * j + 32, :], zcol[:, 4 * a + j, :], sig[b][:, 4 * a + j, :],
                                    start=(a == 0), stop=(a == 1), skip_group_check=True)
                ins.then_inc(den_done, 1)

            def spread(n):
                b, h = divmod(n, HEADS)
                if h == 0:
                    pe.wait_ge(rrow_ready, b + 1)
                if n >= 2:
                    pe.wait_ge(qn_ready, n - 1)
                pe.matmul(ps_bc[n % 2][:, :], pick[:, h:h + 1].broadcast_to([P, P]), rrow[:, :], start=True,
                          stop=True).then_inc(bc_done, 1)

            def fold(h):
                pe.wait_ge(wos_ready, h + 1)
                if h == 0:
                    pe.wait_ge(m_in, 16)
                    pe.wait_ge(full_ready, TILES)
                if h >= 2:
                    pe.wait_ge(mwl_ready, h - 1)
                pe.matmul(ps_t[h % 2][:, :], mT[:, h, :], ring[:, slot(f"wo{h}"), 0:HID], start=True,
                          stop=True).then_inc(mw_done, 1)

            def project(t, heads):
                b, tt = divmod(t, TPB)
                if heads[0] == 0:
                    if t == 0:
                        pe.wait_ge(mwl_ready, HEADS)
                        pe.wait_ge(sig_ready, UNITS)
                    if t >= 2:
                        pe.wait_ge(og_ready, t - 1)
                    pe.wait_ge(ql_ready, HEADS * (b + 1))
                cols = slice(tt * P, (tt + 1) * P)
                for h in heads:
                    for a, w in ((0, 0), (0, 1), (1, 0)):
                        lhs = (qhi if a == 0 else ql)[b][:, h, cols]
                        ins = pe.matmul(ps_main[t % 2][:, :], lhs, MW[:, w, h, :],
                                        start=(h == 0 and a == 0 and w == 0), stop=(h == HEADS - 1 and a == 1))
                if heads[-1] == HEADS - 1:
                    ins.then_inc(o_done, 1)

            def ffn(t):
                pe.wait_ge(lo_ready, TILES + t + 1)
                if t == 0:
                    pe.wait_ge(fwl_ready, KC)
                    pe.wait_ge(const, 8)
                if t == 1:
                    pe.wait_ge(qn_ready, UNITS)
                if t >= 2:
                    pe.wait_ge(fg_ready, 2 * (t - 1))
                if t == 0:
                    pe.wait_ge(brow_ready, 1)
                for half in (1, 0):
                    dst = ps_ffn[t % 2][half][:, 0:FH]
                    cols = slice(half * FH, (half + 1) * FH)
                    pe.matmul(dst, pick_b[:, 0:1].broadcast_to([P, P]), brow[:, cols], start=True, stop=False)
                    for k in range(KC):
                        pe.matmul(dst, h2[:, t % 2, 0, k, :], fhi[:, k, cols], start=False, stop=False)
                        pe.matmul(dst, h2[:, t % 2, 0, k, :], flo(k)[:, cols], start=False, stop=False)
                        ins = pe.matmul(dst, h2[:, t % 2, 1, k, :], fhi[:, k, cols], start=False, stop=(k == KC - 1))
                    ins.then_inc(fr_done if half else f_done, 1)

            def hw_transpose(t):
                pe.wait_ge(hw_ready, t + 1)
                if t == 0:
                    pe.wait_ge(gate_ready, 2 * B)
                else:
                    pe.wait_ge(hwl_ready, t)
                pe.transpose(ps_mod[:, 0:P], hw, ident[:, :]).then_inc(hwT_done, 1)

            def lora(t):
                pe.wait_ge(hwl_ready, t + 1)
                if t == 0:
                    pe.wait_ge(lbl_ready, 1)
                for dst, cols in ((ps_ffn[t % 2][0][:, 0:FH], slice(0, FH)), (ps_ffn[t % 2][1][:, 0:FB], slice(FH, HID))):
                    for a, w in ((0, 0), (0, 1), (1, 0)):
                        ins = pe.matmul(dst, hwT[:, a, :], lbs[w][:, cols], start=False, stop=True, skip_group_check=True)
                ins.then_inc(l_done, 1)

            for t in range(TPB):
                ln1_transpose(t)
            mod_rows(0)
            mod_rows(1)
            mod_transpose(0)
            mod_transpose(1)
            for u in range(UNITS):
                query(u)
                if u < 2:
                    ln1_transpose(TPB + 2 * u)
                    ln1_transpose(TPB + 2 * u + 1)
                if u == 2:
                    mod_rows(2)
                if u == 3:
                    gate_rows(0, 2)
                    gate_rows(1, 2)
                if 5 <= u < 13:
                    fold(u - 5)
                if u in (5, 8):
                    den(0, (u - 5) // 3)
                if 11 <= u < 15:
                    spread(2 * (u - 11))
                    spread(2 * (u - 11) + 1)
                if u in (12, 14):
                    mod_rows(3 + (u - 12) // 2)
                if u == 13:
                    mod_transpose(3)
                    den(1, 0)
            mod_transpose(4)
            den(1, 1)
            first, last = range(0, HEADS // 2), range(HEADS // 2, HEADS)
            for s in range(TILES + 3):
                if s < TILES:
                    project(s, first)
                    if s in (1, 2):
                        spread(6 + 4 * s)
                        spread(7 + 4 * s)
                    project(s, last)
                    if s < 2:
                        spread(8 + 4 * s)
                        spread(9 + 4 * s)
                if s == 0:
                    mod_rows(5)
                if s in (1, 2):
                    gate_rows(s + 1, 5)
                if s == TILES:
                    ffn(s - 2)
                if 0 <= s - 1 < TILES:
                    ln2_transpose(s - 1)
                if 0 <= s - 3 < TILES:
                    hw_transpose(s - 3)
                if 0 <= s - 2 < TILES and s != TILES:
                    ffn(s - 2)
                if 0 <= s - 3 < TILES:
                    lora(s - 3)


def kernel(**inputs):
    import numpy as np
    import concourse.bacc as bacc
    from concourse import mybir as _mybir
    from concourse.bass_utils import run_bass_kernel_spmd

    def arr(name):
        return np.asarray(inputs[name])

    heads = slice(0, None, G)
    dram = {
        "x": arr("L0_attn_hidden_states").reshape(TILES, P, HID),
        "c": arr("L0_c").reshape(B, KC, P).transpose(2, 1, 0),
        "wmod": arr("L0_wmod").reshape(KC, P, 6, HID).transpose(2, 1, 0, 3).reshape(6, P, KC * HID),
        "wq": arr("L0_attn_Wq").reshape(HEADS * G, D, KC, P)[heads].reshape(2, 4, D, KC, P)
        .transpose(0, 4, 1, 3, 2).reshape(2, P, 4 * KC * D),
        "bq": arr("L0_attn_bq").reshape(HEADS * G, D)[heads].T,
        "z": arr("L0_attn_z").T,
        "wo": arr("L0_attn_Wo").reshape(HID, HEADS, G, D).transpose(1, 3, 2, 0).reshape(HEADS, D, G * HID),
        "m": arr("L0_attn_M").transpose(2, 0, 1),
        "fw": np.concatenate([arr("L0_ffn_base_W"), arr("L0_ffn_A").reshape(ER, HID), arr("L0_ffn_router_W")], 0)
        .T.reshape(KC, P, FW - 1).transpose(1, 0, 2),
        "lb": arr("L0_ffn_B").transpose(0, 2, 1).reshape(ER, HID),
        "bb": arr("L0_ffn_base_b").reshape(1, HID),
        "rb": arr("L0_ffn_router_b").reshape(1, NR),
        "map": arr("L0_ffn_expert_map").reshape(1, NR),
    }
    nc = bacc.Bacc("TRN2", target_bir_lowering=False, num_devices=1)
    arrays, args = {}, []
    for name, a in dram.items():
        a = np.ascontiguousarray(a)
        arrays[f"{name}_dram"] = a
        args.append(nc.dram_tensor(f"{name}_dram", a.shape, _mybir.dt.from_np(a.dtype), kind="ExternalInput").ap())
    out = nc.dram_tensor("out_dram", (TILES, P, HID), _mybir.dt.float32, kind="ExternalOutput").ap()
    build(nc, *args, out)
    r = run_bass_kernel_spmd(nc, [arrays], core_ids=[0])
    return r.results[0]["out_dram"].reshape(B, S, HID)
```

```python
from contextlib import ExitStack

import concourse.bass as bass
from concourse import mybir

F32 = mybir.dt.float32
F32R = mybir.dt.float32r
I32 = mybir.dt.int32
ALU = mybir.AluOpType
ACT = mybir.ActivationFunctionType
AX = mybir.AxisListType

P = 128
B, S, HID = 2, 512, 512
HEADS, D = 8, 128
G = 4
KC = HID // P
TILES = B * S // P
TPB = TILES // B
UNITS = B * HEADS
E, R = 8, 16
NR = 2 * E - 1
ER = E * R
FW = HID + ER + NR + 1
FH = FW // 2
FB = HID - FH
EPS_DEN = 1e-6
EPS_LN = 1e-5
GATE_MIN = 0.25
SCALING = 2.0
RING = 3
SLOT = G * HID
MODS = [("sa", 0), ("ca", 1), ("ga", 2), ("sb", 3), ("cb", 4), ("gb", 5)]
MOD_STEPS = {2: 2, 8: 3, 10: 4, 15: 5}
LN1_STEPS = {5: (4, 5), 6: (6, 7)}
FOLD_STEPS = {8: (0, 1), 9: (2,), 10: (3,), 11: (4,), 12: (5,), 13: (6,), 14: (7,)}
ITEMS = ["mod0", "mod1", "wq0", "mod2", "wq1", "wo0", "wo1", "wo2", "mod3", "wo3", "wo4", "mod4", "wo5", "wo6",
         "wo7", "fw0", "mod5", "fw1", "lb"]


def build(nc, x_d, c_d, wmod_d, wq_d, bq_d, z_d, wo_d, m_d, fw_d, lb_d, bb_d, rb_d, map_d, out_d):
    with ExitStack() as ctx:
        def sb(name, shape, dt=F32):
            return ctx.enter_context(nc.sbuf_tensor(name, shape, dt))

        def sem(name):
            return ctx.enter_context(nc.semaphore(name))

        x_sb = sb("x_sb", [P, TILES, HID])
        hn = sb("hn", [P, 2, HID])
        hfull = sb("hfull", [P, 2, HID])
        HT = sb("HT", [P, B, 2, KC, S], F32R)
        WQ = sb("WQ", [P, 2, HEADS, KC, D], F32R)
        sig, ql = [], []
        for b in range(B):
            at = nc.sbuf_base
            sig.append(sb(f"sig{b}", [P, HEADS, S]))
            ql.append(nc.alloc_sbuf_tensor_at(f"ql{b}", [P, HEADS, S], F32R, offset=at))
        MW_hi = sb("MW_hi", [P, HEADS, HID], F32R)
        at = nc.sbuf_base
        wosum = sb("wosum", [P, HEADS, HID])
        MW = [MW_hi, nc.alloc_sbuf_tensor_at("MW_lo", [P, HEADS, HID], F32R, offset=at)]
        ring = sb("ring", [P, RING, SLOT])
        mT = sb("mT", [P, HEADS, D])
        lb_hi = sb("lb_hi", [P, HID], F32R)
        ident = sb("ident", [P, P])
        zcol = sb("zcol", [P, HEADS, 32])
        rfull = sb("rfull", [P, S])
        rrow = sb("rrow", [P, S], F32R)
        gates = sb("gates", [P, 2, B, HID])
        mrow = sb("mrow", [P, HID])
        rden_hi = sb("rden_hi", [P, TPB, 4, 2], F32R)
        et = sb("et", [P, 2, S])
        brow = sb("brow", [P, FW], F32R)
        picks = sb("picks", [P, HEADS + B + 1], F32R)
        pick = picks[:, 0:HEADS]
        pick_g = picks[:, HEADS:HEADS + B]
        pick_b = picks[:, HEADS + B:HEADS + B + 1]
        msk = sb("msk", [P, 8])
        sct = sb("sct", [P, KC, 32])
        cin = sb("cin", [P, KC, B])
        ce = sb("ce", [P, 3, KC, B])
        zin = sb("zin", [P, HEADS])
        bqs = sb("bqs", [P, 3, HEADS])
        mods = sb("mods", [P, 4, KC, B])
        stat = sb("stat", [P, TILES, 2, 6])
        mv = sb("mv", [P, 2, TILES, 2])
        rs = sb("rs", [P, 2, 4, TILES])
        mapi = sb("mapi", [P, NR], I32)
        mapf = sb("mapf", [P, NR])
        oneh = sb("oneh", [P, E, NR])
        sm = sb("sm", [P, 2, 4, 16])
        sms = sb("sms", [P, 2, 4, 8])
        wt = sb("wt", [P, E, NR])
        rden = wt[:, :, :].rearrange("p e r -> p (e r)")[:, 0:TPB * HEADS] \
            .rearrange("p (c j a) -> p c j a", c=TPB, j=4)
        hw = rfull[:, 0:ER]
        hwT = rrow[:, :].rearrange("p (a l t) -> p a l t", a=2, l=2)
        HTf = HT[:, :, :, :, :].rearrange("p b l k s -> p b (l k s)")
        WQf = WQ[:, :, :, :, :].rearrange("p l h k d -> p (l h k d)")
        qhi = [HTf[:, 0, :].rearrange("p (h s) -> p h s", h=HEADS),
               WQf[:, 0:HEADS * S].rearrange("p (h s) -> p h s", h=HEADS)]
        h2 = HTf[:, 1, 0:2 * 2 * HID].rearrange("p (a l k t) -> p a l k t", a=2, l=2, k=KC)
        fhi = WQf[:, HEADS * S:HEADS * S + KC * FW].rearrange("p (k n) -> p k n", k=KC)
        flo3 = HTf[:, 1, 4 * HID:4 * HID + 3 * FW].rearrange("p (k n) -> p k n", k=3)
        flo1 = WQf[:, HEADS * S + KC * FW:HEADS * S + (KC + 1) * FW]
        lbs = [lb_hi[:, :], WQf[:, HEADS * S + (KC + 1) * FW:HEADS * S + (KC + 1) * FW + HID]]
        braw = sig[1][:, HEADS - 2:HEADS, :].rearrange("p h s -> p (h s)")[:, 0:FW]

        def ln_tile(n):
            return sig[1][:, n - 2, :] if n in (2, 3, 6, 7) else hn[:, n % 2, :]

        def flo(k):
            return flo3[:, k, :] if k < 3 else flo1

        bank = [ctx.enter_context(nc.psum_tensor(f"bank{i}", [P, 512], F32)) for i in range(8)]
        ps_main = [bank[0], bank[1]]
        ps_den = bank[2]
        ps_bc = [bank[3], bank[4]]
        ps_t = [bank[5], bank[6]]
        ps_h = bank[3:7]
        ps_mod = bank[7]
        ps_ffn = [[bank[5], bank[6]], [bank[3], bank[4]]]

        def mod_bank(i):
            return (ps_den if i == 1 else ps_mod)[:, :]

        def mod_row(i):
            return (rfull if i == 1 else rrow if i in (2, 5) else mrow)[:, :]

        def gate_bank(n):
            return [ps_den, ps_mod, ps_mod, ps_t[0]][n]

        def ffn_bank(t):
            return ps_main if t == TILES - 2 else ps_ffn[t % 2 if t < TILES - 2 else 0]

        def ffn_et(t):
            return 0 if t == TILES - 2 else 1

        def bc_bank(n):
            if n in (10, 13):
                return ps_mod
            return ps_bc[(n + 1) % 2 if n in (11, 12) else n % 2]

        x_in = [sem(f"x_in{t}") for t in range(TILES)]
        ring_in = [sem(f"ring_in{s}") for s in range(RING)]
        c_in, z_in, bq_in, m_in, map_in = sem("c_in"), sem("z_in"), sem("bq_in"), sem("m_in"), sem("map_in")
        bias_in = sem("bias_in")
        const = sem("const")
        ec_ready, silu_ready = sem("ec_ready"), sem("silu_ready")
        setup = sem("setup")
        mask_ready, zcol_ready, brow_ready = sem("mask_ready"), sem("zcol_ready"), sem("brow_ready")
        mod_done, mrow_ready, modT_done, mods_ready = sem("mod_done"), sem("mrow_ready"), sem("modT_done"), sem("mods_ready")
        grow_ready = sem("grow_ready")
        gate_done, gate_ready = sem("gate_done"), sem("gate_ready")
        st_ready, newton = sem("st_ready"), sem("newton")
        full_dve = sem("full_dve")
        hn_ready, t_done, full_ready, hi_ready, lo_ready = sem("hn_ready"), sem("t_done"), sem("full_ready"), sem("hi_ready"), sem("lo_ready")
        wq_first = sem("wq_first")
        wqh_ready, wql_ready = sem("wqh_ready"), sem("wql_ready")
        q_done, neg_ready, e_ready, bq_ready, sig_ready = sem("q_done"), sem("neg_ready"), sem("e_ready"), sem("bq_ready"), sem("sig_ready")
        den_done, den_sb, denT_done = sem("den_done"), sem("den_sb"), sem("denT_done")
        rfull_zero, r_ready, rT_done, rrow_ready = sem("rfull_zero"), sem("r_ready"), sem("rT_done"), sem("rrow_ready")
        bc_done, qn_ready, qh_act, qh_pool = sem("bc_done"), sem("qn_ready"), sem("qh_act"), sem("qh_pool")
        ql_ready, ql_pool = sem("ql_ready"), sem("ql_pool")
        woa_ready, wos_ready, mw_done, mwh_ready, mwl_ready = sem("woa_ready"), sem("wos_ready"), sem("mw_done"), sem("mwh_ready"), sem("mwl_ready")
        fwh_ready, fwl_ready, lbh_ready, lbl_ready = sem("fwh_ready"), sem("fwl_ready"), sem("lbh_ready"), sem("lbl_ready")
        o_done, og_ready, x2_ready = sem("o_done"), sem("og_ready"), sem("x2_ready")
        fr_done, f_done, rmax_ready, rexp_ready, hw_ready = sem("fr_done"), sem("f_done"), sem("rmax_ready"), sem("rexp_ready"), sem("hw_ready")
        hwT_done, hwh_ready, hwl_ready, l_done = sem("hwT_done"), sem("hwh_ready"), sem("hwl_ready"), sem("l_done")
        fg_ready, res_ready, res_last, out_in = sem("fg_ready"), sem("res_ready"), sem("res_last"), sem("out_in")
        block = ctx.enter_context(nc.Block())

        item = {name: i for i, name in enumerate(ITEMS)}

        def slot(name):
            return item[name] % RING

        def landed(eng, name):
            eng.wait_ge(ring_in[item[name] % RING], 16 * (item[name] // RING + 1))

        @block.sync
        def _(sp):
            def released(name):
                i = int(name[-1]) if name != "lb" else 0
                if name.startswith("mod"):
                    sp.wait_ge(mod_done, i + 1)
                elif name.startswith("wq"):
                    sp.wait_ge(wqh_ready, 4 * i + 4)
                    sp.wait_ge(wql_ready, 4 * i + 4)
                elif name.startswith("wo"):
                    sp.wait_ge(wos_ready, i + 1)
                elif name.startswith("fw"):
                    sp.wait_ge(fwh_ready, i + 1)
                    sp.wait_ge(fwl_ready, 2 * i + 2)

            def load(name):
                n = item[name]
                if n >= RING:
                    released(ITEMS[n - RING])
                dst = ring[:, n % RING, :]
                i = int(name[-1]) if name != "lb" else 0
                if name.startswith("mod"):
                    src = wmod_d[MODS[i][1]]
                elif name.startswith("wq"):
                    src = wq_d[i]
                elif name.startswith("wo"):
                    src = wo_d[i]
                elif name.startswith("fw"):
                    dst = dst[:, 0:2 * FW].rearrange("p (k n) -> p k n", k=2)[:, :, 0:FW - 1]
                    src = fw_d[:, 2 * i:2 * i + 2, :]
                else:
                    dst, src = dst[:, 0:HID], lb_d
                if name == "wq0":
                    dst, src = dst[:, 2 * KC * D:SLOT], src[:, 2 * KC * D:SLOT]
                sp.dma_start(dst, src).then_inc(ring_in[n % RING], 16)

            sp.dma_start(cin[:, :, :], c_d).then_inc(c_in, 16)
            for t in range(TPB):
                sp.dma_start(x_sb[:, t, :], x_d[t]).then_inc(x_in[t], 16)
            load("mod0")
            load("mod1")
            sp.dma_start(ring[:, slot("wq0"), 0:2 * KC * D], wq_d[0][:, 0:2 * KC * D]).then_inc(wq_first, 16)
            for t in range(TPB, TILES):
                sp.dma_start(x_sb[:, t, :], x_d[t]).then_inc(x_in[t], 16)
            load("wq0")
            sp.dma_start(bqs[:, 0, :], bq_d).then_inc(bq_in, 16)
            sp.dma_start(zin[:, :], z_d).then_inc(z_in, 16)
            load("mod2")
            load("wq1")
            sp.dma_start(mT[:, :, :], m_d).then_inc(m_in, 16)
            sp.dma_start(mapi[:, :], map_d.broadcast_to([P, NR])).then_inc(map_in, 16)
            for name in ITEMS[5:]:
                load(name)
            for t in range(TILES):
                if t < TILES - 1:
                    sp.wait_ge(res_ready, t + 1)
                else:
                    sp.wait_ge(res_last, 1)
                sp.dma_start(out_d[t], x_sb[:, t, :]).then_inc(out_in, 16)
            sp.wait_ge(out_in, 16 * TILES)

        @block.gpsimd
        def _(pool):
            pool.memset(sct[:, :, :], 0.0).then_inc(const, 1)
            pool.memset(ident[:, :], 0.0).then_inc(const, 1)
            pool.wait_ge(const, 2)
            pool.affine_select(out=ident[:, :], in_=ident[:, :], compare_op=ALU.not_equal, fill=1.0, base=0,
                               pattern=[[-1, P]], channel_multiplier=1).then_inc(const, 1)
            pool.memset(zcol[:, :, :], 0.0).then_inc(const, 1)
            pool.memset(braw, 0.0).then_inc(const, 1)
            pool.wait_ge(const, 5)
            for p in (0, 32):
                pool.dma_start(braw[p:p + 1, 0:HID], bb_d).then_inc(bias_in, 16)
                pool.dma_start(braw[p:p + 1, HID + ER:HID + ER + NR], rb_d).then_inc(bias_in, 16)

            def wq_hi(h):
                if h == 0:
                    pool.wait_ge(wq_first, 16)
                elif h in (2, 4):
                    landed(pool, f"wq{h // 4}")
                src = ring[:, slot(f"wq{h // 4}"), :].rearrange("p (h n) -> p h n", h=4)[:, h % 4, :]
                pool.tensor_scalar(WQ[:, 0, h, :, :].rearrange("p k d -> p (k d)"), src, 1.0, 1.0,
                                   ALU.mult, ALU.mult).then_inc(wqh_ready, 1)

            def wq_lo(h):
                pool.wait_ge(wqh_ready, h + 1)
                src = ring[:, slot(f"wq{h // 4}"), :].rearrange("p (h n) -> p h n", h=4)[:, h % 4, :]
                hi, lo = (WQ[:, l, h, :, :].rearrange("p k d -> p (k d)") for l in range(2))
                pool.tensor_tensor(lo, src, hi.bitcast(F32), ALU.subtract).then_inc(wql_ready, 1)

            def q_split(n):
                b, h = divmod(n, HEADS)
                if h == 1:
                    pool.wait_ge(q_done, HEADS * (b + 1))
                pool.wait_ge(qn_ready, n + 1)
                pool.tensor_scalar(qhi[b][:, h, :], sig[b][:, h, :], 1.0, 1.0, ALU.mult, ALU.mult).then_inc(qh_pool, 1)
                pool.wait_ge(qh_pool, n // 2 + 1)
                pool.tensor_tensor(ql[b][:, h, :], sig[b][:, h, :], qhi[b][:, h, :].bitcast(F32),
                                   ALU.subtract).then_inc(ql_pool, 1)

            def q_lo(n):
                b, h = divmod(n, HEADS)
                pool.wait_ge(qh_act, n // 2 + 1)
                pool.tensor_tensor(ql[b][:, h, :], sig[b][:, h, :], qhi[b][:, h, :].bitcast(F32),
                                   ALU.subtract).then_inc(ql_pool, 1)

            def wo_sum(h):
                landed(pool, f"wo{h}")
                w = ring[:, slot(f"wo{h}"), :]
                pool.tensor_tensor(w[:, 0:2 * HID], w[:, 0:2 * HID], w[:, 2 * HID:4 * HID], ALU.add).then_inc(woa_ready, 1)
                pool.wait_ge(woa_ready, h + 1)
                pool.tensor_tensor(wosum[:, h, :], w[:, 0:HID], w[:, HID:2 * HID], ALU.add).then_inc(wos_ready, 1)

            for h in range(HEADS):
                wq_hi(h)
                wq_lo(h)
            for h in range(HEADS):
                wo_sum(h)
            for n in range(1, HEADS, 2):
                q_split(n)
            pool.wait_ge(q_done, UNITS)
            pool.memset(fhi[:, :, FW - 1:FW].bitcast(F32), 0.0).then_inc(const, 1)
            pool.memset(flo3[:, :, FW - 1:FW].bitcast(F32), 0.0).then_inc(const, 1)
            pool.memset(flo1[:, FW - 1:FW].bitcast(F32), 0.0).then_inc(const, 1)
            for i in range(2):
                landed(pool, f"fw{i}")
                src = ring[:, slot(f"fw{i}"), 0:2 * FW].rearrange("p (k n) -> p k n", k=2)[:, :, 0:FW - 1]
                pool.tensor_scalar(fhi[:, 2 * i:2 * i + 2, 0:FW - 1], src, 1.0, 1.0, ALU.mult, ALU.mult).then_inc(fwh_ready, 1)
            for k in range(KC):
                pool.wait_ge(fwh_ready, k // 2 + 1)
                raw = ring[:, slot(f"fw{k // 2}"), 0:2 * FW].rearrange("p (k n) -> p k n", k=2)[:, k % 2, 0:FW - 1]
                pool.tensor_tensor(flo(k)[:, 0:FW - 1], raw, fhi[:, k, 0:FW - 1].bitcast(F32),
                                   ALU.subtract).then_inc(fwl_ready, 1)
            landed(pool, "lb")
            pool.tensor_scalar(lbs[0], ring[:, slot("lb"), 0:HID], 1.0, 1.0, ALU.mult, ALU.mult).then_inc(lbh_ready, 1)
            pool.wait_ge(lbh_ready, 1)
            pool.tensor_tensor(lbs[1], ring[:, slot("lb"), 0:HID], lbs[0].bitcast(F32), ALU.subtract).then_inc(lbl_ready, 1)
            for n in range(HEADS + 1, UNITS, 2):
                q_lo(n - 1)
                q_split(n)
            for t in range(TILES - 1):
                pool.wait_ge(fg_ready, 2 * t + 2)
                pool.tensor_tensor(x_sb[:, t, :], et[:, ffn_et(t), :], x_sb[:, t, :], ALU.add).then_inc(res_ready, 1)

        @block.scalar
        def _(act):
            act.wait_ge(c_in, 16)
            act.activation(ce[:, 0, :, :], cin[:, :, :], ACT.Exp, scale=-1.0).then_inc(ec_ready, 1)

            def mod_evac(i):
                act.wait_ge(mod_done, i + 1)
                if i in (3, 4):
                    act.wait_ge(modT_done, {3: 1, 4: 3}[i])
                if i == 5:
                    act.wait_ge(bc_done, HEADS)
                act.activation(mod_row(i), mod_bank(i), ACT.Copy).then_inc(mrow_ready, 1)

            def modulate(n, layer, b, k, dst, src):
                return act.activation(dst, src, ACT.Identity, bias=mods[:, 2 * layer, k, b:b + 1],
                                      scale=mods[:, 2 * layer + 1, k, b:b + 1])

            def ln1_chunk(n):
                b, k = divmod(n, KC)
                act.wait_ge(t_done, TPB * (b + 1))
                act.wait_ge(mods_ready, 2)
                act.wait_ge(lo_ready, n - 1)
                modulate(n, 0, b, k, hfull[:, n % 2, :], ps_h[k][:, :]).then_inc(full_ready, 1)
                if b == 0:
                    return
                act.wait_ge(full_ready, n - 1)
                act.activation(HT[:, b, 0, k, :], hfull[:, n % 2, :], ACT.Copy).then_inc(hi_ready, 1)

            def ln2_tile(t):
                n = TILES + t
                act.wait_ge(t_done, n + 1)
                act.wait_ge(mods_ready, 4)
                act.wait_ge(lo_ready, n - 1)
                if t >= 2:
                    act.wait_ge(f_done, t - 1)
                for k in range(KC):
                    ins = modulate(n, 1, t // TPB, k, hfull[:, n % 2, k * P:(k + 1) * P], ps_den[:, k * P:(k + 1) * P])
                ins.then_inc(full_ready, 1)
                act.wait_ge(full_ready, n - 1)
                act.activation(h2[:, t % 2, 0, :, :].rearrange("p k t -> p (k t)"), hfull[:, n % 2, :],
                               ACT.Copy).then_inc(hi_ready, 1)

            def exp_q(u):
                act.wait_ge(q_done, u + 1)
                if u == 0:
                    act.wait_ge(bq_ready, 1)
                if u >= 2:
                    act.wait_ge(sig_ready, u - 1)
                h = u % HEADS
                act.activation(et[:, u % 2, :], ps_main[u % 2][:, :], ACT.Relu, bias=bqs[:, 2, h:h + 1], scale=-1.0).then_inc(neg_ready, 1)
                act.wait_ge(neg_ready, u + 1)
                act.activation(et[:, u % 2, :], et[:, u % 2, :], ACT.Exp, scale=-1.0).then_inc(e_ready, 1)

            def q_hi(n):
                b, h = divmod(n, HEADS)
                if h == 0:
                    act.wait_ge(q_done, HEADS * (b + 1))
                act.wait_ge(qn_ready, n + 1)
                act.activation(qhi[b][:, h, :], sig[b][:, h, :], ACT.Copy).then_inc(qh_act, 1)

            def den_rows(b):
                act.wait_ge(den_done, 2 * b + 2)
                if b == 0:
                    act.wait_ge(t_done, TILES)
                act.activation(hn[:, 0, :], ps_den[:, :], ACT.Copy).then_inc(den_sb, 1)

            def r_rows(b):
                act.wait_ge(rT_done, b + 1)
                act.wait_ge(gate_done, 2 * b + 2)
                act.activation(rrow[:, :], ps_den[:, :], ACT.Copy).then_inc(rrow_ready, 1)

            def mw_hi(h):
                act.wait_ge(mw_done, h + 1)
                act.activation(MW[0][:, h, :], ps_t[h % 2][:, :], ACT.Copy).then_inc(mwh_ready, 1)

            def hw_hi(t):
                act.wait_ge(hwT_done, t + 1)
                if t >= 2:
                    act.wait_ge(l_done, t - 1)
                act.activation(hwT[:, t % 2, 0, :], ps_mod[:, 0:P], ACT.Copy).then_inc(hwh_ready, 1)

            def route_exp(t):
                act.wait_ge(rmax_ready, t + 1)
                act.activation(sm[:, t % 2, 0, 0:NR], ffn_bank(t)[1][:, FB + ER:FB + ER + NR], ACT.Exp,
                               bias=sms[:, t % 2, 0, 0:1], accum_out=sms[:, t % 2, 0, 1:2]).then_inc(rexp_ready, 1)

            mod_evac(0)
            mod_evac(1)
            act.wait_ge(t_done, TPB)
            act.wait_ge(mods_ready, 2)
            for k in range(KC):
                modulate(k, 0, 0, k, HT[:, 0, 0, k, :], ps_h[k][:, :]).then_inc(hi_ready, 1)
            ln1_chunk(2)
            ln1_chunk(3)
            for u in range(UNITS):
                if u == 9:
                    den_rows(0)
                if u in MOD_STEPS:
                    mod_evac(MOD_STEPS[u])
                for h in FOLD_STEPS.get(u - 1, ()):
                    mw_hi(h)
                if u == 10:
                    r_rows(0)
                exp_q(u)
                for n in LN1_STEPS.get(u, ()):
                    ln1_chunk(n)
                if 11 <= u < 15:
                    q_hi(2 * (u - 11))

            for s in range(TILES):
                if s in (0, 1):
                    (den_rows, r_rows)[s](1)
                if s in (2, 3):
                    q_hi(4 * s)
                    q_hi(4 * s + 2)
                if s >= 1:
                    ln2_tile(s - 1)
                if s >= 3:
                    hw_hi(s - 3)
                if s >= 2:
                    route_exp(s - 2)
            ln2_tile(TILES - 1)
            hw_hi(TILES - 3)
            route_exp(TILES - 2)
            route_exp(TILES - 1)
            hw_hi(TILES - 2)
            hw_hi(TILES - 1)

        @block.vector
        def _(dve):
            steps = [0]

            def step(ins):
                steps[0] += 1
                ins.then_inc(setup, 1)
                dve.wait_ge(setup, steps[0])

            dve.wait_ge(ec_ready, 1)
            step(dve.tensor_scalar(ce[:, 1, :, :], ce[:, 0, :, :], 1.0, None, ALU.add))
            step(dve.reciprocal(ce[:, 2, :, :], ce[:, 1, :, :]))
            dve.wait_ge(const, 1)
            for i in range(2):
                dve.tensor_tensor(sct[:, :, i * B:(i + 1) * B], cin[:, :, :], ce[:, 2, :, :], ALU.mult).then_inc(silu_ready, 1)

            def stats(n, layer, t):
                dve.bn_stats(stat[:, t, layer, :], x_sb[:, t, :]).then_inc(st_ready, 1)
                dve.wait_ge(st_ready, 2 * n + 1)
                dve.bn_aggr(mv[:, layer, t, :], stat[:, t, layer, :]).then_inc(st_ready, 1)

            def rsqrt(n, layer, lo, hi):
                v, hv, y, t = (rs[:, layer, i, lo:hi] for i in (0, 1, 2, 3))
                step(dve.tensor_scalar(v, mv[:, layer, lo:hi, 1], EPS_LN, None, ALU.add))
                step(dve.tensor_scalar(hv, v, -0.5, None, ALU.mult))
                step(dve.tensor_scalar(t.bitcast(I32), v.bitcast(I32), 1, None, ALU.logical_shift_right))
                step(dve.tensor_scalar(y.bitcast(I32), t.bitcast(I32), -1.0, float(0x5F3759DF), ALU.mult, ALU.add))
                for i in range(3):
                    if hi - lo == 1:
                        step(dve.scalar_tensor_tensor(out=t, in0=y, scalar=hv, in1=y, op0=ALU.mult, op1=ALU.mult))
                    else:
                        step(dve.tensor_tensor(t, y, y, ALU.mult))
                        step(dve.tensor_tensor(t, t, hv, ALU.mult))
                    ins = dve.scalar_tensor_tensor(out=y, in0=t, scalar=1.5, in1=y, op0=ALU.add, op1=ALU.mult)
                    if i < 2:
                        step(ins)
                ins.then_inc(newton, 1)
                dve.wait_ge(newton, n + 1)

            def apply(n, layer, t):
                if n in (4, 5):
                    dve.wait_ge(t_done, n - 3)
                if n >= TILES:
                    dve.wait_ge(t_done, n - 1)
                dve.tensor_scalar(ln_tile(n), x_sb[:, t, :], mv[:, layer, t, 0:1], rs[:, layer, 2, t:t + 1],
                                  ALU.subtract, ALU.mult).then_inc(hn_ready, 1)

            def split_lo(n, dst):
                dve.wait_ge(hi_ready, n + 1)
                dve.tensor_tensor(dst[1], hfull[:, n % 2, :], dst[0].bitcast(F32), ALU.subtract).then_inc(lo_ready, 1)

            def ln1_full(k):
                dve.wait_ge(hi_ready, k + 1)
                dve.tensor_scalar(hfull[:, k, :], ps_h[k][:, :], mods[:, 1, k, 0:1], mods[:, 0, k, 0:1],
                                  ALU.mult, ALU.add).then_inc(full_dve, 1)
                dve.wait_ge(full_dve, k + 1)

            def ln1_lo(n):
                if n in (2, 3):
                    dve.wait_ge(full_ready, n - 1)
                split_lo(n, [HT[:, n // KC, l, n % KC, :] for l in range(2)])

            def ln2_lo(t):
                split_lo(TILES + t, [h2[:, t % 2, l, :, :].rearrange("p k t -> p (k t)") for l in range(2)])

            def mod_finish(i, n):
                dve.wait_ge(modT_done, n + 1)
                src = mod_bank([0, 1, 3, 4][i]).rearrange("p (k q r) -> p k r q", k=KC, q=4)[:, :, 0:B, :]
                dst = mods[:, i, :, :]
                if i % 2 == 0:
                    dve.tensor_reduce(dst, src, AX.X, ALU.add).then_inc(mods_ready, 1)
                else:
                    step(dve.tensor_reduce(dst, src, AX.X, ALU.add))
                    dve.tensor_scalar(dst, dst, 1.0, None, ALU.add).then_inc(mods_ready, 1)

            def gate_split(i):
                dve.wait_ge(mrow_ready, i + 1)
                dve.scalar_tensor_tensor(out=rrow[:, :], in0=rrow[:, :].bitcast(F32), scalar=msk[:, 0:1],
                                         in1=mod_bank(i), op0=ALU.mult, op1=ALU.add).then_inc(grow_ready, 1)

            def gate_finish(n):
                dve.wait_ge(gate_done, n + 1)
                src = gate_bank(n)
                g, b = divmod(n, 2)
                dst = gates[:, g, b, :]
                tmp = et[:, 0, :] if g else rfull[:, :]
                step(dve.tensor_scalar(dst, src[:, :], 0.0, 0.5, ALU.is_ge, ALU.subtract))
                step(dve.scalar_tensor_tensor(out=tmp, in0=src[:, :], scalar=4.0, in1=dst, op0=ALU.mult, op1=ALU.mult))
                dve.scalar_tensor_tensor(out=dst, in0=tmp, scalar=2.0 * GATE_MIN, in1=dst, op0=ALU.max,
                                         op1=ALU.mult).then_inc(gate_ready, 1)

            def sig_q(u):
                b, h = divmod(u, HEADS)
                dve.wait_ge(e_ready, u + 1)
                dve.scalar_tensor_tensor(out=sig[b][:, h, :], in0=ps_main[u % 2][:, :], scalar=bqs[:, 1, h:h + 1],
                                         in1=et[:, u % 2, :], op0=ALU.add, op1=ALU.max).then_inc(sig_ready, 1)

            def recip(b):
                dve.wait_ge(denT_done, b + 1)
                r, hi = rden, rden_hi[:, :, :, :]
                dst = rfull[:, :].rearrange("p (c j i) -> p c j i", c=TPB, j=4)
                step(dve.tensor_scalar(r, ps_den[:, :].rearrange("p (c j i) -> p c j i", c=TPB, j=4)[:, :, :, 0:2],
                                       EPS_DEN, None, ALU.add))
                step(dve.reciprocal(r, r))
                step(dve.tensor_scalar(hi, r, 1.0, None, ALU.mult))
                dve.tensor_scalar(dst[:, :, :, 0:2], hi.bitcast(F32), 1.0, None, ALU.mult).then_inc(r_ready, 1)
                dve.tensor_tensor(dst[:, :, :, 2:4], r, hi.bitcast(F32), ALU.subtract).then_inc(r_ready, 1)

            def q_norm(n):
                b, h = divmod(n, HEADS)
                dve.wait_ge(bc_done, n + 1)
                dve.tensor_tensor(sig[b][:, h, :], sig[b][:, h, :], bc_bank(n)[:, :], ALU.mult).then_inc(qn_ready, 1)

            def q_lo(n):
                b, h = divmod(n, HEADS)
                dve.wait_ge(qh_act, n // 2 + 1)
                dve.tensor_tensor(ql[b][:, h, :], sig[b][:, h, :], qhi[b][:, h, :].bitcast(F32), ALU.subtract).then_inc(ql_ready, 1)

            def mw_lo(h):
                dve.wait_ge(mwh_ready, h + 1)
                dve.tensor_tensor(MW[1][:, h, :], ps_t[h % 2][:, :], MW[0][:, h, :].bitcast(F32), ALU.subtract).then_inc(mwl_ready, 1)

            for t in range(TPB):
                dve.wait_ge(x_in[t], 16)
                stats(t, 0, t)
            dve.wait_ge(st_ready, 2 * TPB)
            rsqrt(0, 0, 0, TPB)
            for t in range(TPB):
                apply(t, 0, t)
            dve.wait_ge(const, 3)
            idq = ident[:, :].rearrange("p (j i) -> p j i", j=4)
            for a in range(2):
                step(dve.tensor_tensor(pick[:, 4 * a:4 * a + 4], idq[:, :, a], idq[:, :, a + 2], ALU.add))
            step(dve.tensor_reduce(msk[:, 2:3], idq[:, :, 2:4], AX.XY, ALU.add))
            step(dve.tensor_scalar(msk[:, 0:1], msk[:, 2:3], -1.0, None, ALU.mult))
            step(dve.tensor_scalar(msk[:, 1:2], ident[:, 32:33], -1.0, None, ALU.mult))
            for b in range(B):
                step(dve.tensor_reduce(msk[:, 4:5], idq[:, :, b:b + 3:2], AX.XY, ALU.add))
                step(dve.tensor_copy(pick_g[:, b:b + 1], msk[:, 4:5]))
            dve.tensor_tensor(pick_b[:, 0:1], ident[:, 0:1], ident[:, 32:33], ALU.add).then_inc(mask_ready, 1)
            mod_finish(0, 0)
            mod_finish(1, 1)
            dve.wait_ge(mods_ready, 2)
            for k in range(2):
                ln1_full(k)
                ln1_lo(k)
            ln1_lo(2)
            ln1_lo(3)
            dve.wait_ge(bq_in, 16)
            step(dve.tensor_scalar(bqs[:, 1, :], bqs[:, 0, :], 1.0, None, ALU.add))
            dve.tensor_scalar(bqs[:, 2, :], bqs[:, 0, :], -1.0, None, ALU.mult).then_inc(bq_ready, 1)

            def x_stats(*tiles):
                for t in tiles:
                    dve.wait_ge(x_in[t], 16)
                    stats(t, 0, t)

            x_stats(4, 5)
            for u in range(UNITS):
                for h in FOLD_STEPS.get(u - 1, ()):
                    mw_lo(h)
                if u in (2, 15):
                    gate_split(2 if u == 2 else 5)
                if u in (9, 12):
                    mod_finish(u // 3 - 1, u // 3 - 1)
                if u in (3, 4):
                    apply(2 * u - 2, 0, 2 * u - 2)
                    apply(2 * u - 1, 0, 2 * u - 1)
                if u == 8:
                    dve.wait_ge(gate_ready, B)
                    dve.memset(rfull[:, :], 0.0).then_inc(rfull_zero, 1)
                    dve.wait_ge(rfull_zero, 1)
                if u == 9:
                    recip(0)
                if 11 <= u < 15:
                    q_norm(2 * (u - 11))
                    q_norm(2 * (u - 11) + 1)
                if 12 <= u:
                    q_lo(2 * (u - 12))
                sig_q(u)
                if u == 1:
                    x_stats(6, 7)
                if u == 2:
                    dve.wait_ge(st_ready, 2 * TILES)
                    rsqrt(1, 0, TPB, TILES)
                if u == 10:
                    dve.wait_ge(bias_in, 64)
                    step(dve.tensor_scalar(brow[:, :], braw, 1.0, None, ALU.mult))
                    dve.scalar_tensor_tensor(out=brow[:, :], in0=brow[:, :].bitcast(F32), scalar=msk[:, 1:2], in1=braw,
                                             op0=ALU.mult, op1=ALU.add).then_inc(brow_ready, 1)
                    dve.wait_ge(brow_ready, 1)
                if u == 4:
                    dve.wait_ge(z_in, 16)
                    dve.wait_ge(const, 4)
                    for a in range(2):
                        dve.tensor_copy(zcol[:, 4 * a:4 * a + 4, a::2],
                                        zin[:, 4 * a:4 * a + 4].unsqueeze(2).broadcast_to([P, 4, 16])).then_inc(zcol_ready, 1)
                if u in (4, 5):
                    gate_finish(u - 4)
                for n in LN1_STEPS.get(u, ()):
                    ln1_lo(n)
                if u == 8:
                    dve.wait_ge(map_in, 16)
                    step(dve.tensor_copy(mapf[:, :], mapi[:, :]))
                    for e in range(E):
                        step(dve.tensor_scalar(oneh[:, e, :], mapf[:, :], float(e), None, ALU.is_equal))

            def attn_out(t):
                b = t // TPB
                dve.wait_ge(o_done, t + 1)
                if t == 0:
                    dve.wait_ge(gate_ready, 2 * B)
                dve.tensor_tensor(et[:, 0, :], ps_main[t % 2][:, :], gates[:, 0, b, :], ALU.mult).then_inc(og_ready, 1)
                dve.wait_ge(og_ready, t + 1)
                dve.tensor_tensor(x_sb[:, t, :], et[:, 0, :], x_sb[:, t, :], ALU.add).then_inc(x2_ready, 1)
                dve.wait_ge(x2_ready, t + 1)

            def route_max(t):
                dve.wait_ge(fr_done, t + 1)
                dve.tensor_reduce(sms[:, t % 2, 0, 0:1], ffn_bank(t)[1][:, FB + ER:FB + ER + NR], AX.X, ALU.max,
                                  negate=True).then_inc(rmax_ready, 1)

            def route_weights(t):
                ex, rest, top = (sm[:, t % 2, i, 0:NR] for i in range(3))
                top8, w8, w8s = (sms[:, t % 2, i, :] for i in (1, 2, 3))
                dve.wait_ge(rexp_ready, t + 1)
                step(dve.reciprocal(sms[:, t % 2, 0, 2:3], sms[:, t % 2, 0, 1:2]))
                step(dve.max(top8, ex))
                step(dve.match_replace(rest, top8, ex, 0.0))
                step(dve.tensor_tensor(top, ex, rest, ALU.subtract))
                step(dve.tensor_tensor(wt[:, :, :], oneh[:, :, :], top.unsqueeze(1).broadcast_to([P, E, NR]), ALU.mult))
                step(dve.tensor_reduce(w8, wt[:, :, :], AX.X, ALU.add))
                step(dve.tensor_scalar(w8s, w8, sms[:, t % 2, 0, 2:3], SCALING, ALU.mult, ALU.mult))
                if t == 0:
                    dve.wait_ge(rT_done, B)
                else:
                    dve.wait_ge(hwT_done, t)
                dve.tensor_tensor(hw.rearrange("p (e r) -> p e r", e=E),
                                  ffn_bank(t)[1][:, FB:FB + ER].rearrange("p (e r) -> p e r", e=E),
                                  w8s.unsqueeze(2).broadcast_to([P, E, R]), ALU.mult).then_inc(hw_ready, 1)

            def hw_lo(t):
                dve.wait_ge(hwh_ready, t + 1)
                dve.tensor_tensor(hwT[:, t % 2, 1, :], ps_mod[:, 0:P], hwT[:, t % 2, 0, :].bitcast(F32), ALU.subtract).then_inc(hwl_ready, 1)

            def ffn_out(t):
                b = t // TPB
                tmp = et[:, ffn_et(t), :]
                dve.wait_ge(l_done, t + 1)
                if t >= 1 and t != TILES - 2:
                    dve.wait_ge(res_ready, min(t, TILES - 2))
                dve.tensor_tensor(tmp[:, 0:FH], ffn_bank(t)[0][:, 0:FH], gates[:, 1, b, 0:FH], ALU.mult).then_inc(fg_ready, 1)
                dve.tensor_tensor(tmp[:, FH:HID], ffn_bank(t)[1][:, 0:FB], gates[:, 1, b, FH:HID], ALU.mult).then_inc(fg_ready, 1)
                if t == TILES - 1:
                    dve.wait_ge(fg_ready, 2 * TILES)
                    dve.tensor_tensor(x_sb[:, t, :], tmp, x_sb[:, t, :], ALU.add).then_inc(res_last, 1)

            for s in range(TILES):
                if s == 0:
                    gate_finish(2)
                    gate_finish(3)
                    recip(1)
                attn_out(s)
                stats(TILES + s, 1, s)
                dve.wait_ge(st_ready, 2 * (TILES + s + 1))
                if s == TILES - 1:
                    ln2_lo(s - 1)
                if s >= 3:
                    hw_lo(s - 3)
                rsqrt(2 + s, 1, s, s + 1)
                apply(TILES + s, 1, s)
                if 1 <= s < TILES - 1:
                    ln2_lo(s - 1)
                for n in {1: (8, 9, 10), 2: (11, 12, 13)}.get(s, ()):
                    q_norm(n)
                if s >= 2:
                    route_max(s - 2)
                if s == 2:
                    q_norm(14)
                    q_norm(15)
                if s >= 3:
                    ffn_out(s - 3)
                if s >= 2:
                    route_weights(s - 2)
            ln2_lo(TILES - 1)
            route_max(TILES - 2)
            hw_lo(TILES - 3)
            route_weights(TILES - 2)
            route_max(TILES - 1)
            route_weights(TILES - 1)
            hw_lo(TILES - 2)
            ffn_out(TILES - 3)
            hw_lo(TILES - 1)
            ffn_out(TILES - 2)
            ffn_out(TILES - 1)

        @block.tensor
        def _(pe):
            def mod_rows(i):
                landed(pe, f"mod{i}")
                if i == 0:
                    pe.wait_ge(silu_ready, 2)
                if i in (2, 4, 5):
                    pe.wait_ge(mods_ready, {2: 1, 4: 3, 5: 4}[i])
                if i == 3:
                    pe.wait_ge(gate_ready, B)
                w = ring[:, slot(f"mod{i}"), :].rearrange("p (k n) -> p k n", k=KC)
                for k in range(KC):
                    ins = pe.matmul(mod_bank(i)[32 * k:32 * k + 32, :], sct[:, k, :], w[:, k, :], start=True, stop=True,
                                    skip_group_check=True)
                ins.then_inc(mod_done, 1)

            def mod_transpose(i):
                pe.wait_ge(mrow_ready, i + 1)
                for k in range(KC):
                    ins = pe.transpose(mod_bank(i)[:, k * P:(k + 1) * P], mod_row(i)[:, k * P:(k + 1) * P], ident[:, :])
                ins.then_inc(modT_done, 1)

            def gate_rows(n):
                pe.wait_ge(grow_ready, n // B + 1)
                if n == 0:
                    pe.wait_ge(mask_ready, 1)
                    pe.wait_ge(mods_ready, 2)
                if n == 3:
                    pe.wait_ge(mwl_ready, HEADS - 1)
                b = n % 2
                pe.matmul(gate_bank(n)[:, :], pick_g[:, b:b + 1].broadcast_to([P, P]), rrow[:, :], start=True,
                          stop=True).then_inc(gate_done, 1)

            def ln1_transpose(t):
                pe.wait_ge(hn_ready, t + 1)
                if t >= TPB:
                    pe.wait_ge(full_dve, 2)
                    pe.wait_ge(full_ready, KC - 2)
                if t == 0:
                    pe.wait_ge(const, 3)
                for k in range(KC):
                    ins = pe.transpose(ps_h[k][:, (t % TPB) * P:(t % TPB + 1) * P], ln_tile(t)[:, k * P:(k + 1) * P],
                                       ident[:, :])
                ins.then_inc(t_done, 1)

            def ln2_transpose(t):
                pe.wait_ge(hn_ready, TILES + t + 1)
                if t == 0:
                    pe.wait_ge(rrow_ready, 2)
                else:
                    pe.wait_ge(full_ready, TILES + t - 2)
                for k in range(KC):
                    ins = pe.transpose(ps_den[:, k * P:(k + 1) * P], ln_tile(TILES + t)[:, k * P:(k + 1) * P], ident[:, :])
                ins.then_inc(t_done, 1)

            def query(u, half):
                b, h = divmod(u, HEADS)
                if half == 0:
                    if b == 0:
                        pe.wait_ge(wql_ready, h + 1)
                    if u >= 2:
                        pe.wait_ge(sig_ready, u - 1)
                for k in range(KC):
                    if h == 0:
                        pe.wait_ge(lo_ready if half else hi_ready, KC * b + k + 1)
                    for w in range(1 if half else 2):
                        ins = pe.matmul(ps_main[u % 2][:, :], WQ[:, w, h, k, :], HT[:, b, half, k, :],
                                        start=(half == 0 and k == 0 and w == 0), stop=(half == 1 and k == KC - 1))
                if half == 1:
                    ins.then_inc(q_done, 1)

            def den(b, a):
                pe.wait_ge(sig_ready, HEADS * b + 4 * a + 4)
                if a == 0:
                    if b == 0:
                        pe.wait_ge(zcol_ready, 2)
                        pe.wait_ge(gate_ready, 1)
                    else:
                        pe.wait_ge(rrow_ready, 1)
                for j in range(4):
                    ins = pe.matmul(ps_den[32 * j:32 * j + 32, :], zcol[:, 4 * a + j, :], sig[b][:, 4 * a + j, :],
                                    start=(a == 0), stop=(a == 1), skip_group_check=True)
                ins.then_inc(den_done, 1)

            def den_transpose(b):
                pe.wait_ge(den_sb, b + 1)
                for c in range(TPB):
                    ins = pe.transpose(ps_den[:, c * P:(c + 1) * P], hn[:, 0, c * P:(c + 1) * P], ident[:, :])
                ins.then_inc(denT_done, 1)

            def r_transpose(b):
                pe.wait_ge(r_ready, 2 * b + 2)
                for c in range(TPB):
                    ins = pe.transpose(ps_den[:, c * P:(c + 1) * P], rfull[:, c * P:(c + 1) * P], ident[:, :])
                ins.then_inc(rT_done, 1)

            def spread(n):
                b, h = divmod(n, HEADS)
                if h == 0:
                    pe.wait_ge(rrow_ready, b + 1)
                if n == 10:
                    pe.wait_ge(gate_ready, 2 * B)
                elif n >= 2:
                    pe.wait_ge(qn_ready, n - 2 if n > 10 else n - 1)
                pe.matmul(bc_bank(n)[:, :], pick[:, h:h + 1].broadcast_to([P, P]), rrow[:, :], start=True,
                          stop=True).then_inc(bc_done, 1)

            def fold(h):
                pe.wait_ge(wos_ready, h + 1)
                if h == 0:
                    pe.wait_ge(m_in, 16)
                    pe.wait_ge(full_ready, TILES - 2)
                if h >= 2:
                    pe.wait_ge(mwl_ready, h - 1)
                pe.matmul(ps_t[h % 2][:, :], mT[:, h, :], wosum[:, h, :], start=True,
                          stop=True).then_inc(mw_done, 1)

            def project(t, heads):
                b, tt = divmod(t, TPB)
                if heads[0] == 0:
                    if t == 0:
                        pe.wait_ge(sig_ready, UNITS - 1)
                    if t == 1:
                        pe.wait_ge(sig_ready, UNITS)
                    if t >= 2:
                        pe.wait_ge(og_ready, t - 1)
                if t == 0:
                    pe.wait_ge(mwl_ready, heads[-1] + 1)
                    pe.wait_ge(ql_ready, (heads[-1] + 1) // 2)
                if tt == 0:
                    pe.wait_ge(ql_pool, HEADS // 2 + heads[-1] + 1 if b else (heads[-1] + 1) // 2)
                cols = slice(tt * P, (tt + 1) * P)
                for h in heads:
                    for a, w in ((0, 0), (0, 1), (1, 0)):
                        lhs = (qhi if a == 0 else ql)[b][:, h, cols]
                        ins = pe.matmul(ps_main[t % 2][:, :], lhs, MW[w][:, h, :],
                                        start=(h == 0 and a == 0 and w == 0), stop=(h == HEADS - 1 and a == 1))
                if heads[-1] == HEADS - 1:
                    ins.then_inc(o_done, 1)

            def ffn(t, half):
                if half == 1:
                    pe.wait_ge(lo_ready, TILES + t + 1)
                    if t == 0:
                        pe.wait_ge(fwl_ready, KC)
                        pe.wait_ge(const, 8)
                    if t == 1:
                        pe.wait_ge(qn_ready, UNITS)
                    if t == TILES - 2:
                        pe.wait_ge(og_ready, TILES)
                    elif t >= 2:
                        pe.wait_ge(fg_ready, 2 * (min(t, TILES - 2) - 1))
                    if t == 0:
                        pe.wait_ge(brow_ready, 1)
                dst = ffn_bank(t)[half][:, 0:FH]
                cols = slice(half * FH, (half + 1) * FH)
                pe.matmul(dst, pick_b[:, 0:1].broadcast_to([P, P]), brow[:, cols], start=True, stop=False)
                for k in range(KC):
                    pe.matmul(dst, h2[:, t % 2, 0, k, :], fhi[:, k, cols], start=False, stop=False)
                    pe.matmul(dst, h2[:, t % 2, 0, k, :], flo(k)[:, cols], start=False, stop=False)
                    ins = pe.matmul(dst, h2[:, t % 2, 1, k, :], fhi[:, k, cols], start=False, stop=(k == KC - 1))
                ins.then_inc(fr_done if half else f_done, 1)

            def hw_transpose(t):
                pe.wait_ge(hw_ready, t + 1)
                if t == 0:
                    pe.wait_ge(qn_ready, 14)
                else:
                    pe.wait_ge(hwl_ready, t)
                pe.transpose(ps_mod[:, 0:P], hw, ident[:, :]).then_inc(hwT_done, 1)

            def lora(t):
                pe.wait_ge(hwl_ready, t + 1)
                if t == 0:
                    pe.wait_ge(lbl_ready, 1)
                for dst, cols in ((ffn_bank(t)[0][:, 0:FH], slice(0, FH)), (ffn_bank(t)[1][:, 0:FB], slice(FH, HID))):
                    for a, w in ((0, 0), (0, 1), (1, 0)):
                        ins = pe.matmul(dst, hwT[:, t % 2, a, :], lbs[w][:, cols], start=False, stop=True, skip_group_check=True)
                ins.then_inc(l_done, 1)

            pe.wait_ge(const, 3)
            for i in range(4):
                pe.matmul(ps_main[0][:, :], ident[:, :], ident[:, 0:1].broadcast_to([P, S]), start=True, stop=True)
            mod_rows(0)
            ln1_transpose(0)
            ln1_transpose(1)
            mod_rows(1)
            mod_transpose(0)
            ln1_transpose(2)
            mod_transpose(1)
            ln1_transpose(3)
            query(0, 0)
            query(1, 0)
            query(0, 1)
            query(1, 1)
            for u in range(1, UNITS):
                if u >= 2:
                    query(u, 0)
                    if u == 9:
                        den_transpose(0)
                    if u == 10:
                        r_transpose(0)
                    query(u, 1)
                if u in (3, 15):
                    for n in range(B):
                        gate_rows(n if u == 3 else B + n)
                if u + 1 in MOD_STEPS:
                    mod_rows(MOD_STEPS[u + 1])
                if u == 4:
                    for t in range(TPB, TILES):
                        ln1_transpose(t)
                if u == 8:
                    den(0, 0)
                    den(0, 1)
                for h in FOLD_STEPS.get(u, ()):
                    fold(h)
                if u in (8, 11):
                    mod_transpose(u // 3 + 1)
                if 10 <= u < 14:
                    spread(2 * (u - 10))
                    spread(2 * (u - 10) + 1)
                if u == 13:
                    den(1, 0)
            first, last = range(0, HEADS // 2), range(HEADS // 2, HEADS)
            for s in range(TILES):
                project(s, first)
                if s == 0:
                    den(1, 1)
                if s == 1:
                    r_transpose(1)
                project(s, last[:2])
                if s == 0:
                    den_transpose(1)
                if s == 3:
                    spread(14)
                    spread(15)
                project(s, last[2:])
                if s == 1:
                    for n in (8, 9, 10):
                        spread(n)
                if s >= 1:
                    ln2_transpose(s - 1)
                if s >= 2:
                    ffn(s - 2, 1)
                if s >= 3:
                    hw_transpose(s - 3)
                if s >= 2:
                    ffn(s - 2, 0)
                if s == 2:
                    for n in (11, 12, 13):
                        spread(n)
                if s >= 3:
                    lora(s - 3)
            ffn(TILES - 2, 1)
            ln2_transpose(TILES - 1)
            ffn(TILES - 2, 0)
            hw_transpose(TILES - 3)
            ffn(TILES - 1, 1)
            ffn(TILES - 1, 0)
            hw_transpose(TILES - 2)
            lora(TILES - 3)
            hw_transpose(TILES - 1)
            lora(TILES - 2)
            lora(TILES - 1)


def kernel(**inputs):
    import numpy as np
    import concourse.bacc as bacc
    from concourse import mybir as _mybir
    from concourse.bass_utils import run_bass_kernel_spmd

    def arr(name):
        return np.asarray(inputs[name])

    heads = slice(0, None, G)
    dram = {
        "x": arr("L0_attn_hidden_states").reshape(TILES, P, HID),
        "c": arr("L0_c").reshape(B, KC, P).transpose(2, 1, 0),
        "wmod": arr("L0_wmod").reshape(KC, P, 6, HID).transpose(2, 1, 0, 3).reshape(6, P, KC * HID),
        "wq": arr("L0_attn_Wq").reshape(HEADS * G, D, KC, P)[heads].reshape(2, 4, D, KC, P)
        .transpose(0, 4, 1, 3, 2).reshape(2, P, 4 * KC * D),
        "bq": arr("L0_attn_bq").reshape(HEADS * G, D)[heads].T,
        "z": arr("L0_attn_z").T,
        "wo": arr("L0_attn_Wo").reshape(HID, HEADS, G, D).transpose(1, 3, 2, 0).reshape(HEADS, D, G * HID),
        "m": arr("L0_attn_M").transpose(2, 0, 1),
        "fw": np.concatenate([arr("L0_ffn_base_W"), arr("L0_ffn_A").reshape(ER, HID), arr("L0_ffn_router_W")], 0)
        .T.reshape(KC, P, FW - 1).transpose(1, 0, 2),
        "lb": arr("L0_ffn_B").transpose(0, 2, 1).reshape(ER, HID),
        "bb": arr("L0_ffn_base_b").reshape(1, HID),
        "rb": arr("L0_ffn_router_b").reshape(1, NR),
        "map": arr("L0_ffn_expert_map").reshape(1, NR),
    }
    nc = bacc.Bacc("TRN2", target_bir_lowering=False, num_devices=1)
    arrays, args = {}, []
    for name, a in dram.items():
        a = np.ascontiguousarray(a)
        arrays[f"{name}_dram"] = a
        args.append(nc.dram_tensor(f"{name}_dram", a.shape, _mybir.dt.from_np(a.dtype), kind="ExternalInput").ap())
    out = nc.dram_tensor("out_dram", (TILES, P, HID), _mybir.dt.float32, kind="ExternalOutput").ap()
    build(nc, *args, out)
    r = run_bass_kernel_spmd(nc, [arrays], core_ids=[0])
    return r.results[0]["out_dram"].reshape(B, S, HID)
```
